# Optimizing a Trainium2 kernel written in Bass

```python
import numpy as np
import jax
import jax.numpy as jnp

def _softmax(x, axis=-1):
    return jax.nn.softmax(x, axis=axis)

def _gelu(x):
    return jax.nn.gelu(x, approximate=True)

def _silu(x):
    return jax.nn.silu(x)

def _sigmoid(x):
    return jax.nn.sigmoid(x)

def _layernorm(x, axis=-1, eps=1e-05):
    m = jnp.mean(x, axis=axis, keepdims=True)
    v = jnp.var(x, axis=axis, keepdims=True)
    return (x - m) / jnp.sqrt(v + eps)

def _scatter_add(tgt, idx, src, axis=0):
    return tgt.at[idx].add(src)

def _segment_sum(src, seg, n):
    return jax.ops.segment_sum(src, seg, n)
kernel_name = 'mk_gnn_preln_d1_gnn_r8_c4ee98'

def setup_inputs(seed: int=0):
    np.random.seed(seed)
    _w = jnp.asarray

    def _rec_inputs():
        import jax
        import jax.numpy as jnp
        _gk = jax.random.key(seed)
        x = -0.000202 + 1 * jax.random.normal(jax.random.fold_in(_gk, 1), (6250, 128), jnp.float32)
        src = jax.random.randint(jax.random.fold_in(_gk, 2), (200000,), 0, 6250, jnp.int32)
        dst = jnp.minimum((6250 * jax.random.uniform(jax.random.fold_in(_gk, 3), (200000,)) ** 2.0).astype(jnp.int32), 49999)
        _o = jnp.argsort(dst, stable=True)
        src = src[_o]
        dst = dst[_o]
        edge_attr_4 = -0.000107899 + 1.00008 * jax.random.normal(jax.random.fold_in(_gk, 11), (200000, 4), jnp.float32)
        edge_attr_8 = jax.random.uniform(jax.random.fold_in(_gk, 12), (200000, 8), jnp.float32, 0.0, 1)
        return (x, src, dst, edge_attr_4, edge_attr_8)
    x, src, dst, edge_attr_4, edge_attr_8 = _rec_inputs()

    def _L0_gnn_setup():
        import jax, jax.numpy as jnp
        import numpy as np
        MUL = 32
        N_NODES = 6250
        N_EDGES = 100000
        R3 = np.sqrt(3.0).astype(np.float32)
        key = jax.random.key(seed)
        ks = jax.random.split(key, 12)
        inp = {}
        inp['node_feats'] = jax.random.normal(ks[0], (N_NODES, 4 * MUL), dtype=jnp.float32)
        inp['edge_attrs'] = jax.random.normal(ks[1], (N_EDGES, 4), dtype=jnp.float32)
        inp['edge_feats'] = jax.random.uniform(ks[2], (N_EDGES, 8), dtype=jnp.float32)
        inp['edge_index'] = jax.random.randint(ks[3], (2, N_EDGES), 0, N_NODES)
        inp['W_up_s'] = jax.random.normal(ks[4], (MUL, MUL), dtype=jnp.float32)
        inp['W_up_v'] = jax.random.normal(ks[5], (MUL, MUL), dtype=jnp.float32)
        inp['A1'] = jax.random.normal(ks[6], (8, 64), dtype=jnp.float32) / np.sqrt(8.0)
        inp['b1'] = jnp.zeros((64,), dtype=jnp.float32)
        inp['A2'] = jax.random.normal(ks[7], (64, 64), dtype=jnp.float32) / np.sqrt(64.0)
        inp['b2'] = jnp.zeros((64,), dtype=jnp.float32)
        inp['A3'] = jax.random.normal(ks[8], (64, 4 * MUL), dtype=jnp.float32) * (10.0 * np.sqrt(6.0 / (64 + 4 * MUL)))
        inp['W_out_s'] = jax.random.normal(ks[9], (2 * MUL, MUL), dtype=jnp.float32)
        inp['W_out_v'] = jax.random.normal(ks[10], (2 * MUL, MUL), dtype=jnp.float32)
        return inp
    _L0_gnn_all = _L0_gnn_setup()
    _L0_gnn_in = {k: v for k, v in _L0_gnn_all.items() if k in ('W_up_s', 'W_up_v', 'A1', 'b1', 'A2', 'b2', 'A3', 'W_out_s', 'W_out_v')}
    del _L0_gnn_all
    return {'x': x, 'src': src, 'dst': dst, 'edge_attr_4': edge_attr_4, 'edge_attr_8': edge_attr_8, 'L0_gnn_W_up_s': _L0_gnn_in['W_up_s'], 'L0_gnn_W_up_v': _L0_gnn_in['W_up_v'], 'L0_gnn_A1': _L0_gnn_in['A1'], 'L0_gnn_b1': _L0_gnn_in['b1'], 'L0_gnn_A2': _L0_gnn_in['A2'], 'L0_gnn_b2': _L0_gnn_in['b2'], 'L0_gnn_A3': _L0_gnn_in['A3'], 'L0_gnn_W_out_s': _L0_gnn_in['W_out_s'], 'L0_gnn_W_out_v': _L0_gnn_in['W_out_v']}

def reference(x, src, dst, edge_attr_4, edge_attr_8, L0_gnn_W_up_s, L0_gnn_W_up_v, L0_gnn_A1, L0_gnn_b1, L0_gnn_A2, L0_gnn_b2, L0_gnn_A3, L0_gnn_W_out_s, L0_gnn_W_out_v):
    import jax
    import jax.numpy as jnp

    def _L0_gnn_ref(node_feats, edge_attrs, edge_feats, W_up_s, W_up_v, A1, b1, A2, b2, A3, W_out_s, W_out_v, edge_index):
        import jax, jax.numpy as jnp
        import numpy as np
        MUL = 32
        N_NODES = 6250
        N_EDGES = 100000
        R3 = np.sqrt(3.0).astype(np.float32)
        num_nodes = node_feats.shape[0]
        sender, receiver = (edge_index[0], edge_index[1])
        s = node_feats[:, :MUL]
        v = node_feats[:, MUL:].reshape(num_nodes, MUL, 3)
        inv = 1.0 / np.sqrt(MUL).astype(np.float32)
        s = s @ W_up_s * inv
        v = jnp.einsum('nui,uw->nwi', v, W_up_v) * inv
        h = jax.nn.silu(edge_feats @ A1 + b1)
        h = jax.nn.silu(h @ A2 + b2)
        tpw = h @ A3
        w0, w1, w2, w3 = jnp.split(tpw, 4, axis=1)
        ss = s[sender]
        vs = v[sender]
        y_s = edge_attrs[:, :1]
        y_v = edge_attrs[:, 1:4]
        out_s0 = ss * y_s * w0
        out_s3 = jnp.einsum('eui,ei->eu', vs, y_v) / R3 * w3
        out_v1 = ss[:, :, None] * y_v[:, None, :] * w1[:, :, None]
        out_v2 = vs * y_s[:, :, None] * w2[:, :, None]
        E = ss.shape[0]
        mji = jnp.concatenate([out_s0, out_s3, out_v1.reshape(E, 3 * MUL), out_v2.reshape(E, 3 * MUL)], axis=1)
        message = jax.ops.segment_sum(mji, receiver, num_segments=num_nodes) / 10.0
        ms = message[:, :2 * MUL]
        mv = message[:, 2 * MUL:].reshape(num_nodes, 2 * MUL, 3)
        inv2 = 1.0 / np.sqrt(2 * MUL).astype(np.float32)
        out_s = ms @ W_out_s * inv2
        out_v = jnp.einsum('nui,uw->nwi', mv, W_out_v) * inv2
        return jnp.concatenate([out_s, out_v.reshape(num_nodes, 3 * MUL)], axis=1)
    edge_index = jnp.stack([src, dst])
    h = jnp.maximum(_layernorm(x, axis=-1), 0.0)
    x = x + _L0_gnn_ref(h, edge_attr_4, edge_attr_8, L0_gnn_W_up_s, L0_gnn_W_up_v, L0_gnn_A1, L0_gnn_b1, L0_gnn_A2, L0_gnn_b2, L0_gnn_A3, L0_gnn_W_out_s, L0_gnn_W_out_v, edge_index)
    return x

_drawn_inputs = setup_inputs


def setup_inputs(seed=0):
    import zlib

    import numpy as np

    out = dict(_drawn_inputs(seed))
    spreads = {'L0_gnn_b1': (0.0, 0.1), 'L0_gnn_b2': (0.0, 0.1)}
    factors = {}
    for name, (base, spread) in spreads.items():
        noise = np.random.default_rng([zlib.crc32(name.encode()), seed]).standard_normal(out[name].shape)
        drawn = base * np.exp(spread * noise) if base else spread * noise
        out[name] = jnp.asarray(drawn.astype(out[name].dtype))
    for name, factor in factors.items():
        out[name] = (out[name] * factor).astype(out[name].dtype)
    return out
```

```python
from contextlib import ExitStack

import numpy as np
import concourse.bass as bass
from concourse import mybir

F32, I32 = mybir.dt.float32, mybir.dt.int32
ALU, ACT, AX = mybir.AluOpType, mybir.ActivationFunctionType, mybir.AxisListType

P = 128
MUL = 32
F = 4 * MUL
HID = 64
EF = 8
N_NODES, N_EDGES = 6250, 200000
NT = -(-N_NODES // P)
NPAD = NT * P
CT = 7
NCH = NT // CT
PIECES = [(0, 4), (4, 3)]

GROUP = 2 * P
QT = 4
QUADS = 4
TILES = QT * QUADS
BLOCK = TILES * P
BODY = 2
QB = BODY * QUADS
NJ = -(-N_EDGES // (BLOCK * BODY))
NB = NJ * BODY
NW = NB * BLOCK // GROUP
HT = TILES // 2
EPAD = NB * BLOCK
W = 32
GP = 112
ACC = NPAD + W
MAX_ROUNDS = NPAD // W + 1
SLOTS = 2
OUT_N = 448
OUT_STEPS = NPAD // OUT_N
EPS = 1e-5
MLP_HALF = HT * P // 2

MSG_CREDIT = QB
SCATTER_CREDIT = SLOTS
W_CREDIT = QB
ADD_CREDIT = 3
HALF_CREDIT = 2


def gnn_layer_kernel(nc, x, xT, src, dst, dst_groups, attr, efT, Wus, Wuv, A1, b1, A2, b2, A3, Wos, Wov, outT):
    table = nc.dram_tensor("node_table", (NPAD, F), F32, kind="Internal").ap()
    starts_dram = nc.dram_tensor("window_starts", (1, NW), F32, kind="Internal").ap()
    spans_dram = nc.dram_tensor("window_spans", (1, NW), F32, kind="Internal").ap()

    ctx = ExitStack()
    with ctx:
        def sb(name, shape, dt=F32):
            return ctx.enter_context(nc.sbuf_tensor(name, shape, dt))

        def pb(name, shape):
            return ctx.enter_context(nc.psum_tensor(name, shape, F32))

        def sem(name):
            return ctx.enter_context(nc.semaphore(name))

        acc = sb("acc", [P, 4, ACC])
        xT_sb = sb("xT_sb", [P, NPAD])
        center = sb("center", [P, P])
        w_up = sb("w_up", [F, F])
        a1_bd = sb("a1_bd", [2 * EF, 2 * HID])
        a2_bd = sb("a2_bd", [2 * HID, 2 * HID])
        a3_bd = sb("a3_bd", [2 * HID, 2 * F])
        b1_sb = sb("b1_sb", [2 * HID, 1])
        b2_sb = sb("b2_sb", [2 * HID, 1])
        w_out = sb("w_out", [F, 4, F])
        iota_i = sb("iota_i", [P, W], I32)
        iota_f = sb("iota_f", [P, W])
        start_row = sb("start_row", [1, NW])
        start_at = sb("start_at", [1, NW], I32)
        start_all = sb("start_all", [P, NW])
        start_now = sb("start_now", [P, NW])
        span_row = sb("span_row", [1, NW])
        span_max = sb("span_max", [1, 1])
        span_int = sb("span_int", [1, 1], I32)
        span_windows = sb("span_windows", [1, 1], I32)
        rounds_sb = sb("rounds_sb", [1, 1], I32)
        offset = sb("offset", [P, 1])
        group_stats = sb("group_stats", [GP, 2, NW // GP])
        group_span = sb("group_span", [GP, NW // GP])
        bn = sb("bn", [P, NT, 6])
        mean_gap = sb("mean_gap", [P, NT])
        gap_sq = sb("gap_sq", [P, NT])
        m2_sum = sb("m2_sum", [P, NT])
        var_sum = sb("var_sum", [P, NT])
        var_eps = sb("var_eps", [P, NT])
        std = sb("std", [P, NT])
        rstd = sb("rstd", [P, NT])
        rows = sb("rows", [P, QT * QB, F])
        msgs = sb("msgs", [P, SLOTS, QT, 2, F])
        onehot = sb("onehot", [P, 2, HT, 4, W])
        eq = sb("eq", [P, HT, W])
        rel = sb("rel", [P, HT])
        h1 = sb("h1", [2 * HID, 2, MLP_HALF])
        h2 = sb("h2", [2 * HID, BODY, 2, MLP_HALF])
        ef_in = sb("ef_in", [2 * EF, BODY, 2 * MLP_HALF])
        attr_in = sb("attr_in", [P, BODY, TILES * 4])
        dst_in = sb("dst_in", [P, BODY, TILES], I32)
        src_in = sb("src_in", [P, BODY, TILES], I32)
        x_chunk = rows[:, 0:3 * CT, :].rearrange("p (b t) f -> p b t f", b=3)
        relu_c = msgs[:].rearrange("p a b c d -> p (a b c d)")[:, 0:2 * CT * P].rearrange("p (b n) -> p b n", b=2)
        tab_c = onehot[:].rearrange("p a b c d -> p (a b c d)")[:, 0:2 * CT * P].rearrange("p (b t f) -> p b t f", b=2, t=CT)
        dst_g = h2[:].rearrange("p a b c -> p (a b c)")[0:GP, 0:NW // GP * GROUP].bitcast(I32).rearrange("p (g e) -> p g e", e=GROUP)

        ps1 = pb("ps1", [P, 2, 512])
        ps2 = pb("ps2", [P, 2, 512])
        psw = pb("psw", [P, SLOTS, QT, 2, 2, MUL])
        pss = pb("pss", [P, SLOTS, 512])

        dst_loaded = sem("dst_loaded")
        xT_loaded = [sem(f"xT_loaded{c}") for c in range(NCH)]
        x_loaded = [sem(f"x_loaded{i}") for i in range(3)]
        weights_zeroed = sem("weights_zeroed")
        up_loaded = sem("up_loaded")
        weights_loaded = sem("weights_loaded")
        center_built = sem("center_built")
        iota_built = sem("iota_built")
        up_scaled = sem("up_scaled")
        centered = sem("centered")
        relu_done = sem("relu_done")
        up_done = sem("up_done")
        table_piece = sem("table_piece")
        stats_step = sem("stats_step")
        bn_done = sem("bn_done")
        std_done = sem("std_done")
        rstd_done = sem("rstd_done")
        table_stored = [sem(f"table_stored{i}") for i in range(2)]
        groups_reduced = sem("groups_reduced")
        groups_stored = sem("groups_stored")
        groups_back = sem("groups_back")
        rounds_step = sem("rounds_step")
        acc_zeroed = sem("acc_zeroed")
        out_scaled = sem("out_scaled")
        round_step = sem("round_step")
        ef_loaded = [sem(f"ef_loaded{b}") for b in range(BODY)]
        attr_loaded = [sem(f"attr_loaded{b}") for b in range(BODY)]
        src_loaded = [sem(f"src_loaded{b}") for b in range(BODY)]
        gathered = [sem(f"gathered{p}") for p in range(QB)]
        slots_claimed = sem("slots_claimed")
        l1_done = sem("l1_done")
        h1_ready = sem("h1_ready")
        l2_done = sem("l2_done")
        h2_ready = sem("h2_ready")
        w_ready = sem("w_ready")
        msgs_ready = sem("msgs_ready")
        rel_ready = sem("rel_ready")
        eq_ready = sem("eq_ready")
        onehot_ready = sem("onehot_ready")
        scatter_done = sem("scatter_done")
        window_added = sem("window_added")
        out_summed = sem("out_summed")
        out_added = sem("out_added")
        out_stored = sem("out_stored")

        round_sems = [round_step, *ef_loaded, *attr_loaded, *src_loaded, *gathered, slots_claimed, l1_done, h1_ready, l2_done,
                      h2_ready, w_ready, msgs_ready, rel_ready, eq_ready, onehot_ready, scatter_done, window_added]

        with nc.Block() as block:

            @block.sync
            def _(sp):
                sp.dma_start(dst_g, dst_groups).then_inc(dst_loaded, 16)
                for c in range(NCH):
                    cols = slice(c * CT * P, (c + 1) * CT * P)
                    sp.dma_start(xT_sb[:, cols], xT[:, cols]).then_inc(xT_loaded[c], 16)
                    if c >= 3:
                        sp.wait_ge(bn_done, c - 2)
                    sp.dma_start(x_chunk[:, c % 3], x[cols, :].rearrange("(t p) f -> p t f", p=P)).then_inc(x_loaded[c % 3], 16)
                sp.wait_ge(groups_reduced, 3)
                sp.dma_start(starts_dram.rearrange("a (p g) -> (a p) g", p=GP), group_stats[:, 0, :]).then_inc(groups_stored, 16)
                sp.dma_start(spans_dram.rearrange("a (p g) -> (a p) g", p=GP), group_span[:, :]).then_inc(groups_stored, 16)
                sp.wait_ge(groups_stored, 32)
                sp.dma_start(start_row[:, :], starts_dram).then_inc(groups_back, 16)
                sp.dma_start(span_row[:, :], spans_dram).then_inc(groups_back, 16)
                sp.dma_start(start_all[:, :], starts_dram.broadcast_to([P, NW])).then_inc(groups_back, 16)
                for c in range(NCH):
                    sp.wait_ge(table_piece, 2 * (c + 1))
                    sp.dma_start(table[c * CT * P:(c + 1) * CT * P, :].rearrange("(t p) f -> p t f", p=P),
                                 tab_c[:, c % 2]).then_inc(table_stored[c % 2], 16)
                for i in range(2):
                    sp.wait_ge(table_stored[i], 16 * ((NCH + 1 - i) // 2))

            @block.gpsimd
            def _(pool):
                pool.memset(w_up[:, :], 0.0).then_inc(weights_zeroed, 1)
                pool.memset(center[:, :], -1.0 / P).then_inc(center_built, 1)
                pool.wait_ge(center_built, 1)
                pool.affine_select(out=center[:, :], in_=center[:, :], compare_op=ALU.not_equal, fill=1.0 - 1.0 / P,
                                   base=0, pattern=[[-1, P]], channel_multiplier=1).then_inc(center_built, 1)
                pool.memset(a1_bd[:, :], 0.0).then_inc(weights_zeroed, 1)
                pool.memset(a2_bd[:, :], 0.0).then_inc(weights_zeroed, 1)
                pool.memset(a3_bd[:, :], 0.0).then_inc(weights_zeroed, 1)
                pool.memset(w_out[:, :, :], 0.0).then_inc(weights_zeroed, 1)
                pool.iota(iota_i[:, :], pattern=[[1, W]], base=0, channel_multiplier=0).then_inc(iota_built, 1)
                pool.memset(offset[:, :], 0.0).then_inc(iota_built, 1)
                pool.memset(acc[:, :, :], 0.0).then_inc(acc_zeroed, 1)
                pool.wait_ge(acc_zeroed, 1)

            @block.scalar
            def _(act):
                act.wait_ge(weights_zeroed, 1)
                act.dma_start(w_up[0:MUL, 0:MUL], Wus).then_inc(up_loaded, 16)
                for i in range(3):
                    b = slice(MUL * (i + 1), MUL * (i + 2))
                    act.dma_start(w_up[b, b], Wuv).then_inc(up_loaded, 16)
                act.wait_ge(weights_zeroed, 5)
                for g in range(2):
                    h = slice(HID * g, HID * (g + 1))
                    act.dma_start(a1_bd[EF * g:EF * (g + 1), h], A1).then_inc(weights_loaded, 16)
                    act.dma_start(a2_bd[h, h], A2).then_inc(weights_loaded, 16)
                    act.dma_start(a3_bd[h, F * g:F * (g + 1)], A3).then_inc(weights_loaded, 16)
                    act.dma_start(b1_sb[h, :], b1).then_inc(weights_loaded, 16)
                    act.dma_start(b2_sb[h, :], b2).then_inc(weights_loaded, 16)
                v = [slice(MUL * (i + 1), MUL * (i + 2)) for i in range(3)]
                s = slice(0, MUL)
                act.dma_start(w_out[s, 0, s], Wos[0:MUL, :]).then_inc(weights_loaded, 16)
                for i in range(3):
                    act.dma_start(w_out[v[i], 0, v[i]], Wov[MUL:2 * MUL, :]).then_inc(weights_loaded, 16)
                    act.dma_start(w_out[s, 1 + i, v[i]], Wov[0:MUL, :]).then_inc(weights_loaded, 16)
                    act.dma_start(w_out[v[i], 1 + i, s], Wos[MUL:2 * MUL, :]).then_inc(weights_loaded, 16)
                for c in range(NCH):
                    for k, (t0, nt) in enumerate(PIECES):
                        act.wait_ge(centered, 2 * c + k + 1)
                        if c >= 2:
                            act.wait_ge(up_done, 2 * (c - 2) + k + 1)
                        act.activation(relu_c[:, c % 2, t0 * P:(t0 + nt) * P], ps1[:, k, 0:nt * P],
                                       ACT.Relu).then_inc(relu_done, 1)
                    n = slice(c * CT, (c + 1) * CT)
                    act.wait_ge(stats_step, 5 * (c + 1))
                    act.activation(std[:, n], var_eps[:, n], ACT.Sqrt).then_inc(std_done, 1)

            @block.vector
            def _(dve):
                dve.wait_ge(dst_loaded, 16)
                dve.tensor_reduce(group_stats[:, 0, :], dst_g, AX.X, ALU.min).then_inc(groups_reduced, 1)
                dve.tensor_reduce(group_stats[:, 1, :], dst_g, AX.X, ALU.max).then_inc(groups_reduced, 1)
                dve.wait_ge(groups_reduced, 2)
                dve.tensor_tensor(group_span[:, :], group_stats[:, 1, :], group_stats[:, 0, :],
                                  ALU.subtract).then_inc(groups_reduced, 1)
                dve.wait_ge(up_loaded, 64)
                dve.tensor_scalar(w_up[:, :], w_up[:, :], float(MUL) ** -0.5, None, ALU.mult).then_inc(up_scaled, 1)
                dve.wait_ge(iota_built, 2)
                dve.tensor_copy(iota_f[:, :], iota_i[:, :]).then_inc(rounds_step, 1)
                step = 0

                def stats(c):
                    nonlocal step
                    dve.wait_ge(x_loaded[c % 3], 16 * (c // 3 + 1))
                    for t in range(c * CT, (c + 1) * CT):
                        last = dve.bn_stats(bn[:, t, :], x_chunk[:, c % 3, t - c * CT, :])
                    last.then_inc(bn_done, 1)
                    dve.wait_ge(bn_done, c + 1)
                    n = slice(c * CT, (c + 1) * CT)
                    dve.tensor_tensor(mean_gap[:, n], bn[:, n, 1], bn[:, n, 4], ALU.subtract).then_inc(stats_step, 1)
                    dve.tensor_tensor(m2_sum[:, n], bn[:, n, 2], bn[:, n, 5], ALU.add).then_inc(stats_step, 1)
                    step += 2
                    dve.wait_ge(stats_step, step)
                    dve.tensor_tensor(gap_sq[:, n], mean_gap[:, n], mean_gap[:, n], ALU.mult).then_inc(stats_step, 1)
                    step += 1
                    dve.wait_ge(stats_step, step)
                    dve.scalar_tensor_tensor(var_sum[:, n], gap_sq[:, n], F / 4.0, m2_sum[:, n],
                                             ALU.mult, ALU.add).then_inc(stats_step, 1)
                    step += 1
                    dve.wait_ge(stats_step, step)
                    dve.tensor_scalar(var_eps[:, n], var_sum[:, n], 1.0 / F, EPS, ALU.mult, ALU.add).then_inc(stats_step, 1)
                    step += 1

                stats(0)
                for c in range(NCH):
                    if c + 1 < NCH:
                        stats(c + 1)
                    n = slice(c * CT, (c + 1) * CT)
                    dve.wait_ge(std_done, c + 1)
                    dve.reciprocal(rstd[:, n], std[:, n]).then_inc(rstd_done, 1)
                    dve.wait_ge(rstd_done, c + 1)
                    if c >= 2:
                        dve.wait_ge(table_stored[c % 2], 16 * (c // 2))
                    for k, (t0, nt) in enumerate(PIECES):
                        dve.wait_ge(up_done, 2 * c + k + 1)
                        n = slice(c * CT + t0, c * CT + t0 + nt)
                        dve.tensor_tensor(tab_c[:, c % 2, t0:t0 + nt, :],
                                          ps2[:, k, 0:nt * P].rearrange("p (t f) -> p t f", f=F),
                                          rstd[:, n].unsqueeze(2).broadcast_to([P, nt, F]),
                                          ALU.mult).then_inc(table_piece, 1)
                dve.wait_ge(groups_back, 48)
                dve.tensor_reduce(span_max[:, :], span_row[:, :], AX.X, ALU.max).then_inc(rounds_step, 1)
                dve.wait_ge(rounds_step, 2)
                dve.tensor_copy(span_int[:, :], span_max[:, :]).then_inc(rounds_step, 1)
                dve.wait_ge(rounds_step, 3)
                dve.tensor_scalar(span_windows[:, :], span_int[:, :], W.bit_length() - 1, None,
                                  ALU.arith_shift_right).then_inc(rounds_step, 1)
                dve.wait_ge(rounds_step, 4)
                dve.tensor_scalar(rounds_sb[:, :], span_windows[:, :], 1.0, float(MAX_ROUNDS),
                                  ALU.add, ALU.min).then_inc(rounds_step, 1)
                dve.wait_ge(weights_loaded, 16 * 20)
                dve.tensor_scalar(w_out[:, :, :], w_out[:, :, :], 0.1 * (2.0 * MUL) ** -0.5, None,
                                  ALU.mult).then_inc(out_scaled, 1)
                dve.wait_ge(out_scaled, 1)
                for i in range(3):
                    v = slice(MUL * (i + 1), MUL * (i + 2))
                    dve.tensor_scalar(w_out[v, 1 + i, 0:MUL], w_out[v, 1 + i, 0:MUL], 3.0 ** -0.5, None,
                                      ALU.mult).then_inc(out_scaled, 1)
                dve.wait_ge(out_scaled, 4)
                dve.wait_ge(rounds_step, 5)

            @block.tensor
            def _(pe):
                pe.wait_ge(center_built, 2)

                def center_chunk(c):
                    pe.wait_ge(xT_loaded[c], 16)
                    for k, (t0, nt) in enumerate(PIECES):
                        if c >= 1:
                            pe.wait_ge(relu_done, 2 * (c - 1) + k + 1)
                        n0 = (c * CT + t0) * P
                        nc.tensor.matmul(ps1[:, k, 0:nt * P], center[:, :], xT_sb[:, n0:n0 + nt * P],
                                         start=True, stop=True).then_inc(centered, 1)

                def up_chunk(c):
                    for k, (t0, nt) in enumerate(PIECES):
                        pe.wait_ge(relu_done, 2 * c + k + 1)
                        if c >= 1:
                            pe.wait_ge(table_piece, 2 * (c - 1) + k + 1)
                        for t in range(nt):
                            last = nc.tensor.matmul(ps2[:, k, t * P:(t + 1) * P],
                                                    relu_c[:, c % 2, (t0 + t) * P:(t0 + t + 1) * P],
                                                    w_up[:, :], start=True, stop=True)
                        last.then_inc(up_done, 1)

                center_chunk(0)
                pe.wait_ge(up_scaled, 1)
                for c in range(NCH):
                    if c + 1 < NCH:
                        center_chunk(c + 1)
                    up_chunk(c)

        rounds = nc.values_load(rounds_sb[0:1, 0:1], min_val=1, max_val=MAX_ROUNDS)
        with nc.Fori(0, rounds):
            with nc.Block() as block:

                @block.sync
                def _(sp):
                    def load_ef(j, b):
                        sp.dma_start(ef_in[:, b, :], efT[bass.ds(j * BODY + b, 1), :, :].rearrange("a p n -> (a p) n")
                                     ).then_inc(ef_loaded[b], 16)

                    def load_attr(j, b):
                        n = bass.ds(j * BODY + b, 1)
                        sp.dma_start(attr_in[:, b, :], attr[n, :, :].rearrange("a p n -> (a p) n")).then_inc(attr_loaded[b], 16)
                        sp.dma_start(dst_in[:, b, :], dst[n, :, :].rearrange("a p n -> (a p) n")).then_inc(attr_loaded[b], 16)

                    def load_src(j, b):
                        sp.dma_start(src_in[:, b, :], src[bass.ds(j * BODY + b, 1), :, :].rearrange("a p n -> (a p) n")
                                     ).then_inc(src_loaded[b], 16)

                    for b in range(BODY):
                        load_src(0, b)
                        load_ef(0, b)
                        load_attr(0, b)
                    with sp.Fori(0, NJ - 1) as j:
                        for b in range(BODY):
                            sp.wait_ge(l1_done, j * 2 * BODY + 2 * b + 2)
                            load_ef(j + 1, b)
                            sp.wait_ge(onehot_ready, j * 2 * BODY + 2 * b + 2)
                            load_attr(j + 1, b)
                            sp.wait_ge(msgs_ready, j * QB + b * QUADS + QUADS + MSG_CREDIT)
                            load_src(j + 1, b)

                @block.gpsimd
                def _(pool):
                    with pool.Fori(0, NJ) as j:
                        for p in range(QB):
                            b, k = divmod(p, QUADS)
                            if k == 0:
                                pool.wait_ge(src_loaded[b], j * 16 + 16)
                            pool.wait_ge(msgs_ready, j * QB + p + 1)
                            pool.sem_inc(slots_claimed, 1)
                            for t in range(QT):
                                at = QT * k + t
                                pool.indirect_dma_start(
                                    out=rows[:, QT * p + t, :], out_offset=None, in_=table,
                                    in_offset=bass.IndirectOffsetOnAxis(ap=src_in[:, b, at:at + 1], axis=0),
                                ).then_inc(gathered[p], 16)

                @block.scalar
                def _(act):
                    act.sem_inc(h1_ready, HALF_CREDIT)
                    act.sem_inc(h2_ready, HALF_CREDIT)

                    def silu_1(m, h):
                        act.wait_ge(l1_done, m + 1)
                        act.wait_ge(l2_done, m + 1)
                        act.activation(h1[:, h, :], ps1[:, h, :], ACT.Silu, bias=b1_sb[:, 0:1]).then_inc(h1_ready, 1)

                    def silu_2(m, h, b, quads_before):
                        act.wait_ge(l2_done, m + 1 + HALF_CREDIT)
                        act.wait_ge(w_ready, quads_before + QUADS)
                        act.activation(h2[:, b, h, :], ps2[:, h, :], ACT.Silu, bias=b2_sb[:, 0:1]).then_inc(h2_ready, 1)

                    def mlp(j, b):
                        for h in range(2):
                            silu_1(j * 2 * BODY + 2 * b + h, h)
                        for h in range(2):
                            silu_2(j * 2 * BODY + 2 * b + h, h, b, j * QB + b * QUADS)

                    mlp(0, 0)
                    with act.Fori(0, NJ - 1) as j:
                        mlp(j, 1)
                        mlp(j + 1, 0)
                    mlp(NJ - 1, 1)

                @block.vector
                def _(dve):
                    dve.sem_inc(msgs_ready, MSG_CREDIT)
                    dve.sem_inc(window_added, ADD_CREDIT)
                    dve.tensor_scalar(start_now[:, :], start_all[:, :], offset[:, 0:1], None, ALU.add).then_inc(round_step, 1)
                    dve.tensor_scalar(span_row[:, :], start_row[:, :], offset[0:1, 0:1], float(NPAD),
                                      ALU.add, ALU.min).then_inc(round_step, 1)
                    dve.wait_ge(round_step, 2)
                    dve.tensor_scalar(start_at[:, :], span_row[:, :], 0.0, None, ALU.max).then_inc(round_step, 1)
                    dve.tensor_scalar(offset[:, :], offset[:, :], float(W), None, ALU.add).then_inc(round_step, 1)
                    dve.wait_ge(round_step, 4)

                    def relative(j, g):
                        b, h = divmod(g, 2)
                        dve.wait_ge(attr_loaded[b], j * 32 + 32)
                        dve.tensor_tensor(
                            rel[:, :].rearrange("p (w t) -> p w t", t=2),
                            dst_in[:, b, h * HT:(h + 1) * HT].rearrange("p (w t) -> p w t", t=2),
                            start_now[:, bass.ds(j * 2 * QB + g * HT // 2, HT // 2)].unsqueeze(2).broadcast_to([P, HT // 2, 2]),
                            ALU.subtract).then_inc(rel_ready, 1)

                    def equal(j, g):
                        dve.wait_ge(rel_ready, j * 4 + g + 1)
                        dve.tensor_tensor(eq[:, :, :], iota_f[:, :].unsqueeze(1).broadcast_to([P, HT, W]),
                                          rel[:, :].unsqueeze(2).broadcast_to([P, HT, W]),
                                          ALU.is_equal).then_inc(eq_ready, 1)

                    def scale(j, g):
                        b, h = divmod(g, 2)
                        dve.wait_ge(eq_ready, j * 4 + g + 1)
                        dve.tensor_tensor(
                            onehot[:, h, :, :, :],
                            eq[:, :, :].unsqueeze(2).broadcast_to([P, HT, 4, W]),
                            attr_in[:, b, h * 4 * HT:(h + 1) * 4 * HT].rearrange("p (t c) -> p t c", c=4)
                            .unsqueeze(3).broadcast_to([P, HT, 4, W]),
                            ALU.mult).then_inc(onehot_ready, 1)

                    def messages(j, p):
                        dve.wait_ge(gathered[p], j * 16 * QT + 16 * QT)
                        dve.wait_ge(w_ready, j * QB + p + 1 + W_CREDIT)
                        dve.wait_ge(scatter_done, j * QB + p + 1)
                        g = rows[:, QT * p:QT * (p + 1), :].rearrange("p t (c u) -> p t c u", c=4)
                        m = msgs[:, p % SLOTS].rearrange("p t k (c u) -> p t k c u", c=4)
                        w = psw[:, p % SLOTS]
                        dve.tensor_tensor(m[:, :, :, 0, :], g[:, :, 0, :].unsqueeze(2).broadcast_to([P, QT, 2, MUL]),
                                          w[:, :, :, 0, :], ALU.mult)
                        dve.tensor_tensor(m[:, :, :, 1:4, :],
                                          g[:, :, 1:4, :].unsqueeze(2).broadcast_to([P, QT, 2, 3, MUL]),
                                          w[:, :, :, 1, :].unsqueeze(3).broadcast_to([P, QT, 2, 3, MUL]),
                                          ALU.mult).then_inc(msgs_ready, 1)

                    def add_window(j, p, i):
                        n = j * 2 * QB + 2 * p + i
                        start = dve.value_load(start_at[0:1, bass.ds(n, 1)], min_val=0, max_val=NPAD)
                        dve.wait_ge(scatter_done, j * QB + p + 1 + SCATTER_CREDIT)
                        dve.wait_ge(window_added, n + ADD_CREDIT)
                        at = acc[:, :, bass.ds(start, W)]
                        sums = pss[:, p % SLOTS, i * 4 * W:(i + 1) * 4 * W].rearrange("p (c w) -> p c w", c=4)
                        dve.tensor_tensor(at, at, sums, ALU.add).then_inc(window_added, 1)

                    def iteration(j, last):
                        for p in range(QB):
                            g = p // 2 + 1
                            ahead = (j + g // 4, g % 4) if not (last and g == 4) else None
                            messages(j, p)
                            if ahead and p % 2 == 0:
                                relative(*ahead)
                            if p:
                                add_window(j, p - 1, 0)
                            if ahead:
                                (equal, scale)[p % 2](*ahead)
                            if p:
                                add_window(j, p - 1, 1)
                        for i in range(2):
                            add_window(j, QB - 1, i)

                    relative(0, 0)
                    equal(0, 0)
                    scale(0, 0)
                    with dve.Fori(0, NJ - 1) as j:
                        iteration(j, False)
                    iteration(NJ - 1, True)

                @block.tensor
                def _(pe):
                    pe.sem_inc(scatter_done, SCATTER_CREDIT)
                    pe.sem_inc(w_ready, W_CREDIT)
                    pe.sem_inc(l2_done, HALF_CREDIT)

                    def layer_1(j, b, h):
                        m = j * 2 * BODY + 2 * b + h
                        pe.wait_ge(ef_loaded[b], j * 16 + 16)
                        pe.wait_ge(h1_ready, m + 1)
                        nc.tensor.matmul(ps1[:, h, :], a1_bd[:, :], ef_in[:, b, h * MLP_HALF:(h + 1) * MLP_HALF],
                                         start=True, stop=True).then_inc(l1_done, 1)

                    def layer_2(j, b, h):
                        m = j * 2 * BODY + 2 * b + h
                        pe.wait_ge(h1_ready, m + 1 + HALF_CREDIT)
                        pe.wait_ge(h2_ready, m + 1)
                        nc.tensor.matmul(ps2[:, h, :], a2_bd[:, :], h1[:, h, :],
                                         start=True, stop=True).then_inc(l2_done, 1)

                    def layer_3(j, p):
                        b, k = divmod(p, QUADS)
                        h, c = divmod(2 * k, 4)
                        pe.wait_ge(h2_ready, j * 2 * BODY + 2 * b + h + 1 + HALF_CREDIT)
                        pe.wait_ge(msgs_ready, j * QB + p - 1 + MSG_CREDIT)
                        for i in range(2):
                            last = nc.tensor.matmul(
                                psw[:, p % SLOTS, 2 * i:2 * i + 2].rearrange("p b c d e -> p (b c d e)"),
                                h2[:, b, h, (c + i) * P:(c + i + 1) * P], a3_bd[:, :], start=True, stop=True)
                        last.then_inc(w_ready, 1)

                    def scatter(j, p):
                        g, k = divmod(p, 2)
                        pe.wait_ge(msgs_ready, j * QB + p + 1 + MSG_CREDIT)
                        pe.wait_ge(onehot_ready, j * 4 + g + 1)
                        pe.wait_ge(window_added, j * 2 * QB + 2 * p + 1)
                        for i in range(2):
                            for part, c0, c1 in ((0, 0, 1), (1, 1, 4)):
                                for t in (2 * i, 2 * i + 1):
                                    last = nc.tensor.matmul(
                                        pss[:, p % SLOTS, (4 * i + c0) * W:(4 * i + c1) * W],
                                        msgs[:, p % SLOTS, t, part, :],
                                        onehot[:, g % 2, QT * k + t, c0:c1, :].rearrange("p c w -> p (c w)"),
                                        start=(t == 2 * i), stop=(t == 2 * i + 1))
                        last.then_inc(scatter_done, 1)

                    def mlp_part(j, b, part):
                        (layer_1 if part < 2 else layer_2)(j, b, part % 2)

                    def iteration(j, last):
                        for p in range(QB):
                            b, k = divmod(p, QUADS)
                            if p + 1 < QB:
                                layer_3(j, p + 1)
                            elif not last:
                                layer_3(j + 1, 0)
                            if b == 0:
                                mlp_part(j, 1, k)
                            elif not last:
                                mlp_part(j + 1, 0, k)
                            scatter(j, p)

                    for part in range(4):
                        mlp_part(0, 0, part)
                    layer_3(0, 0)
                    with pe.Fori(0, NJ - 1) as j:
                        iteration(j, False)
                    iteration(NJ - 1, True)

            nc.all_engine_barrier()
            for s in round_sems:
                nc.sync.sem_clear(s)
            nc.all_engine_barrier()

        with nc.Block() as block:

            @block.tensor
            def _(pe):
                pe.sem_inc(out_added, 2)
                with pe.Fori(0, OUT_STEPS // 2) as j:
                    for k in range(2):
                        pe.wait_ge(out_added, j * 2 + k + 1)
                        for c in range(4):
                            last = nc.tensor.matmul(ps1[:, k, 0:OUT_N], w_out[:, c, :],
                                                    acc[:, c, bass.ds(j * 2 * OUT_N + k * OUT_N, OUT_N)],
                                                    start=(c == 0), stop=(c == 3))
                        last.then_inc(out_summed, 1)

            @block.vector
            def _(dve):
                with dve.Fori(0, OUT_STEPS // 2) as j:
                    for k in range(2):
                        dve.wait_ge(out_summed, j * 2 + k + 1)
                        at = xT_sb[:, bass.ds(j * 2 * OUT_N + k * OUT_N, OUT_N)]
                        dve.tensor_tensor(at, at, ps1[:, k, 0:OUT_N], ALU.add).then_inc(out_added, 1)

            @block.sync
            def _(sp):
                with sp.Fori(0, OUT_STEPS // 2) as j:
                    for k in range(2):
                        n = bass.ds(j * 2 * OUT_N + k * OUT_N, OUT_N)
                        sp.wait_ge(out_added, j * 2 + k + 1 + 2)
                        sp.dma_start(outT[:, n], xT_sb[:, n]).then_inc(out_stored, 16)
                sp.wait_ge(out_stored, 16 * OUT_STEPS)


FEATURES = np.concatenate([np.arange(MUL)] + [MUL + 3 * np.arange(MUL) + i for i in range(3)])
WEIGHT_COLUMNS = np.concatenate([MUL * k + np.arange(MUL) for k in (0, 2, 1, 3)])


def kernel(x, src, dst, edge_attr_4, edge_attr_8, L0_gnn_W_up_s, L0_gnn_W_up_v, L0_gnn_A1, L0_gnn_b1, L0_gnn_A2,
           L0_gnn_b2, L0_gnn_A3, L0_gnn_W_out_s, L0_gnn_W_out_v):
    import concourse.bacc as bacc
    from concourse.bass_utils import run_bass_kernel_spmd

    x, src, dst = np.asarray(x), np.asarray(src), np.asarray(dst)
    attr, ef = np.asarray(edge_attr_4), np.asarray(edge_attr_8)
    pad = EPAD - N_EDGES
    x_pad = np.pad(x, ((0, NPAD - N_NODES), (0, 0)))
    dst_pad = np.pad(dst, (0, pad), mode="edge")
    tiles = lambda a: np.ascontiguousarray(a.reshape(NB, TILES, P, -1).transpose(0, 2, 1, 3).reshape(NB, P, -1))
    arrays = {
        "x": x_pad,
        "xT": np.ascontiguousarray(x_pad[:, FEATURES].T),
        "src": tiles(np.pad(src, (0, pad))),
        "dst": tiles(dst_pad),
        "dst_groups": dst_pad.reshape(GP, NW // GP, GROUP),
        "attr": tiles(np.pad(attr, ((0, pad), (0, 0)))),
        "efT": np.ascontiguousarray(np.pad(ef, ((0, pad), (0, 0))).reshape(NB, TILES // 2, 2, P, EF)
                                    .transpose(0, 2, 4, 1, 3).reshape(NB, 2 * EF, BLOCK // 2)),
        "Wus": np.asarray(L0_gnn_W_up_s),
        "Wuv": np.asarray(L0_gnn_W_up_v),
        "A1": np.asarray(L0_gnn_A1),
        "b1": np.asarray(L0_gnn_b1).reshape(HID, 1),
        "A2": np.asarray(L0_gnn_A2),
        "b2": np.asarray(L0_gnn_b2).reshape(HID, 1),
        "A3": np.ascontiguousarray(np.asarray(L0_gnn_A3)[:, WEIGHT_COLUMNS]),
        "Wos": np.asarray(L0_gnn_W_out_s),
        "Wov": np.asarray(L0_gnn_W_out_v),
    }
    nc = bacc.Bacc("TRN2", target_bir_lowering=False, num_devices=1)
    args = {n: nc.dram_tensor(f"in_{n}", a.shape, mybir.dt.from_np(a.dtype), kind="ExternalInput").ap()
            for n, a in arrays.items()}
    outT = nc.dram_tensor("out_T", (F, NPAD), F32, kind="ExternalOutput").ap()
    gnn_layer_kernel(nc, **args, outT=outT)
    r = run_bass_kernel_spmd(nc, [{f"in_{n}": a for n, a in arrays.items()}], core_ids=[0])
    got = r.results[0]["out_T"][:, :N_NODES].T
    out = np.empty((N_NODES, F), got.dtype)
    out[:, FEATURES] = got
    return out
```

```python
from contextlib import ExitStack

import numpy as np
import concourse.bass as bass
from concourse import mybir

F32, I32 = mybir.dt.float32, mybir.dt.int32
ALU, ACT, AX = mybir.AluOpType, mybir.ActivationFunctionType, mybir.AxisListType

P = 128
MUL = 32
F = 4 * MUL
HID = 64
EF = 8
N_NODES, N_EDGES = 6250, 200000
NT = -(-N_NODES // P)
NPAD = NT * P
CT = 7
NCH = NT // CT
PIECES = [(0, 4), (4, 3)]

GROUP = 2 * P
QT = 4
QUADS = 4
TILES = QT * QUADS
BLOCK = TILES * P
BODY = 2
QB = BODY * QUADS
NJ = -(-N_EDGES // (BLOCK * BODY))
NB = NJ * BODY
NW = NB * BLOCK // GROUP
HT = TILES // 2
EPAD = NB * BLOCK
W = 32
GP = 112
XW = NPAD + W
MAX_ROUNDS = NPAD // W + 1
SLOTS = 2
OCTS = QB // 2
OW = 4
WINDOW_LAG = 2 * OW
EPS = 1e-5
MLP_HALF = HT * P // 2

N_WEIGHT_LOADS = 20
LAST_EDGES = N_EDGES - (NJ - 1) * BODY * BLOCK
LAST_TILES = -(-LAST_EDGES // P)
LAST_QUADS = -(-LAST_TILES // QT)
LAST_OCT = (LAST_QUADS - 1) // 2

MSG_CREDIT = QB
SCATTER_CREDIT = SLOTS
W_CREDIT = QB
SUMS_CREDIT = 2
OUT_CREDIT = 2
ADD_CREDIT = 2 * OW
HALF_CREDIT = 2


def quad_tiles(p):
    return max(0, min(QT, LAST_TILES - QT * p))


def gnn_layer_kernel(nc, x, xT, src, dst, dst_groups, attr, efT, Wus, Wuv, A1, b1, A2, b2, A3, Wos, Wov, outT):
    table = nc.dram_tensor("node_table", (NPAD, F), F32, kind="Internal").ap()
    starts_dram = nc.dram_tensor("window_starts", (1, NW), F32, kind="Internal").ap()
    spans_dram = nc.dram_tensor("window_spans", (1, NW), F32, kind="Internal").ap()

    ctx = ExitStack()
    with ctx:
        def sb(name, shape, dt=F32):
            return ctx.enter_context(nc.sbuf_tensor(name, shape, dt))

        def pb(name, shape):
            return ctx.enter_context(nc.psum_tensor(name, shape, F32))

        def sem(name):
            return ctx.enter_context(nc.semaphore(name))

        xT_sb = sb("xT_sb", [P, XW])
        center = sb("center", [P, P])
        w_up = sb("w_up", [F, F])
        a1_bd = sb("a1_bd", [2 * EF, 2 * HID])
        a2_bd = sb("a2_bd", [2 * HID, 2 * HID])
        a3_bd = sb("a3_bd", [2 * HID, 2 * F])
        b1_sb = sb("b1_sb", [2 * HID, 1])
        b2_sb = sb("b2_sb", [2 * HID, 1])
        w_out = sb("w_out", [F, 4, F])
        iota_i = sb("iota_i", [P, W], I32)
        iota_f = sb("iota_f", [P, W])
        start_row = sb("start_row", [1, NW])
        start_at = sb("start_at", [1, NW], I32)
        start_all = sb("start_all", [P, NW])
        start_now = sb("start_now", [P, NW])
        span_row = sb("span_row", [1, NW])
        span_max = sb("span_max", [1, 1])
        span_int = sb("span_int", [1, 1], I32)
        span_windows = sb("span_windows", [1, 1], I32)
        rounds_sb = sb("rounds_sb", [1, 1], I32)
        offset = sb("offset", [P, 1])
        group_stats = sb("group_stats", [GP, 2, NW // GP])
        group_span = sb("group_span", [GP, NW // GP])
        bn = sb("bn", [P, NT, 6])
        mean_gap = sb("mean_gap", [P, NT])
        gap_sq = sb("gap_sq", [P, NT])
        m2_sum = sb("m2_sum", [P, NT])
        var_sum = sb("var_sum", [P, NT])
        var_eps = sb("var_eps", [P, NT])
        std = sb("std", [P, NT])
        rstd = sb("rstd", [P, NT])
        rows = sb("rows", [P, QT * QB, F])
        msgs = sb("msgs", [P, SLOTS, QT, 2, F])
        onehot = sb("onehot", [P, 2, HT, 4, W])
        eq = sb("eq", [P, HT, W])
        rel = sb("rel", [P, HT])
        sums = sb("sums", [P, 2, OW, 4, W])
        h1 = sb("h1", [2 * HID, 2, MLP_HALF])
        h2 = sb("h2", [2 * HID, BODY, 2, MLP_HALF])
        ef_in = sb("ef_in", [2 * EF, BODY, 2 * MLP_HALF])
        attr_in = sb("attr_in", [P, BODY, TILES * 4])
        dst_in = sb("dst_in", [P, BODY, TILES], I32)
        src_in = sb("src_in", [P, BODY, TILES], I32)
        x_sb = sb("x_sb", [P, NT, F])
        tab_sb = sb("tab_sb", [P, NT, F])
        relu_c = msgs[:].rearrange("p a b c d -> p (a b c d)")[:, 0:2 * CT * P].rearrange("p (b n) -> p b n", b=2)
        dst_g = h2[:].rearrange("p a b c -> p (a b c)")[0:GP, 0:NW // GP * GROUP].bitcast(I32).rearrange("p (g e) -> p g e", e=GROUP)

        ps1 = pb("ps1", [P, 1, 512])
        ps2 = pb("ps2", [P, 1, 512])
        psw = pb("psw", [P, SLOTS, QT, 2, 2, MUL])
        pss = pb("pss", [P, 2, OW, 4, W])
        pso = pb("pso", [P, 2, 512])
        psc = psw[:].rearrange("p a b c d e -> p a (b c d e)")
        psu = pss[:].rearrange("p a b c d -> p a (b c d)")

        dst_loaded = sem("dst_loaded")
        xT_loaded = [sem(f"xT_loaded{c}") for c in range(NCH)]
        x_loaded = [sem(f"x_loaded{c}") for c in range(NCH)]
        weights_zeroed = sem("weights_zeroed")
        up_loaded = sem("up_loaded")
        weights_loaded = sem("weights_loaded")
        center_built = sem("center_built")
        iota_built = sem("iota_built")
        up_scaled = sem("up_scaled")
        centered = sem("centered")
        relu_done = sem("relu_done")
        up_done = sem("up_done")
        table_piece = sem("table_piece")
        stats_step = sem("stats_step")
        bn_done = sem("bn_done")
        std_done = sem("std_done")
        rstd_done = sem("rstd_done")
        table_stored = sem("table_stored")
        groups_reduced = sem("groups_reduced")
        groups_stored = sem("groups_stored")
        groups_back = sem("groups_back")
        rounds_step = sem("rounds_step")
        edge_zeroed = sem("edge_zeroed")
        out_scaled = sem("out_scaled")
        round_step = sem("round_step")
        ef_loaded = [sem(f"ef_loaded{b}") for b in range(BODY)]
        attr_loaded = [sem(f"attr_loaded{b}") for b in range(BODY)]
        src_loaded = [sem(f"src_loaded{b}") for b in range(BODY)]
        gathered = [sem(f"gathered{p}") for p in range(QB)]
        slots_claimed = sem("slots_claimed")
        l1_done = sem("l1_done")
        h1_ready = sem("h1_ready")
        l2_done = sem("l2_done")
        h2_ready = sem("h2_ready")
        w_ready = sem("w_ready")
        msgs_ready = sem("msgs_ready")
        rel_ready = sem("rel_ready")
        eq_ready = sem("eq_ready")
        onehot_ready = sem("onehot_ready")
        scatter_done = sem("scatter_done")
        sums_copied = sem("sums_copied")
        out_ready = sem("out_ready")
        window_added = sem("window_added")
        out_stored = sem("out_stored")

        round_sems = [round_step, *ef_loaded, *attr_loaded, *src_loaded, *gathered, slots_claimed, l1_done, h1_ready, l2_done,
                      h2_ready, w_ready, msgs_ready, rel_ready, eq_ready, onehot_ready, scatter_done, sums_copied, out_ready,
                      window_added]

        with nc.Block() as block:

            @block.sync
            def _(sp):
                for c in range(NCH):
                    cols = slice(c * CT * P, (c + 1) * CT * P)
                    sp.dma_start(xT_sb[:, cols], xT[:, cols]).then_inc(xT_loaded[c], 16)
                    sp.dma_start(x_sb[:, c * CT:(c + 1) * CT, :],
                                 x[cols, :].rearrange("(t p) f -> p t f", p=P)).then_inc(x_loaded[c], 16)
                    if c == 2:
                        sp.dma_start(dst_g, dst_groups).then_inc(dst_loaded, 16)
                for c in range(NCH):
                    sp.wait_ge(table_piece, 2 * (c + 1))
                    sp.dma_start(table[c * CT * P:(c + 1) * CT * P, :].rearrange("(t p) f -> p t f", p=P),
                                 tab_sb[:, c * CT:(c + 1) * CT, :]).then_inc(table_stored, 16)
                    if c == 3:
                        sp.wait_ge(groups_reduced, 3)
                        sp.dma_start(starts_dram.rearrange("a (p g) -> (a p) g", p=GP),
                                     group_stats[:, 0, :]).then_inc(groups_stored, 16)
                        sp.dma_start(spans_dram.rearrange("a (p g) -> (a p) g", p=GP),
                                     group_span[:, :]).then_inc(groups_stored, 16)
                    if c == 4:
                        sp.wait_ge(groups_stored, 32)
                        sp.dma_start(start_row[:, :], starts_dram).then_inc(groups_back, 16)
                        sp.dma_start(span_row[:, :], spans_dram).then_inc(groups_back, 16)
                        sp.dma_start(start_all[:, :], starts_dram.broadcast_to([P, NW])).then_inc(groups_back, 16)

            @block.gpsimd
            def _(pool):
                pool.memset(w_up[:, :], 0.0).then_inc(weights_zeroed, 1)
                pool.memset(center[:, :], -1.0 / P).then_inc(center_built, 1)
                pool.wait_ge(center_built, 1)
                pool.affine_select(out=center[:, :], in_=center[:, :], compare_op=ALU.not_equal, fill=1.0 - 1.0 / P,
                                   base=0, pattern=[[-1, P]], channel_multiplier=1).then_inc(center_built, 1)
                pool.memset(a1_bd[:, :], 0.0).then_inc(weights_zeroed, 1)
                pool.memset(a2_bd[:, :], 0.0).then_inc(weights_zeroed, 1)
                pool.memset(a3_bd[:, :], 0.0).then_inc(weights_zeroed, 1)
                pool.memset(w_out[:, :, :], 0.0).then_inc(weights_zeroed, 1)
                pool.iota(iota_i[:, :], pattern=[[1, W]], base=0, channel_multiplier=0).then_inc(iota_built, 1)
                pool.memset(offset[:, :], 0.0).then_inc(iota_built, 1)
                pool.memset(xT_sb[:, NPAD:XW], 0.0).then_inc(edge_zeroed, 1)
                pool.wait_ge(weights_zeroed, 5)
                for g in range(2):
                    h = slice(HID * g, HID * (g + 1))
                    pool.dma_start(a1_bd[EF * g:EF * (g + 1), h], A1).then_inc(weights_loaded, 16)
                    pool.dma_start(a2_bd[h, h], A2).then_inc(weights_loaded, 16)
                    pool.dma_start(a3_bd[h, F * g:F * (g + 1)], A3).then_inc(weights_loaded, 16)
                    pool.dma_start(b1_sb[h, :], b1).then_inc(weights_loaded, 16)
                    pool.dma_start(b2_sb[h, :], b2).then_inc(weights_loaded, 16)
                v = [slice(MUL * (i + 1), MUL * (i + 2)) for i in range(3)]
                s = slice(0, MUL)
                pool.dma_start(w_out[s, 0, s], Wos[0:MUL, :]).then_inc(weights_loaded, 16)
                for i in range(3):
                    pool.dma_start(w_out[v[i], 0, v[i]], Wov[MUL:2 * MUL, :]).then_inc(weights_loaded, 16)
                    pool.dma_start(w_out[s, 1 + i, v[i]], Wov[0:MUL, :]).then_inc(weights_loaded, 16)
                    pool.dma_start(w_out[v[i], 1 + i, s], Wos[MUL:2 * MUL, :]).then_inc(weights_loaded, 16)
                pool.wait_ge(weights_loaded, 16 * N_WEIGHT_LOADS)
                pool.wait_ge(edge_zeroed, 1)

            @block.scalar
            def _(act):
                act.wait_ge(weights_zeroed, 1)
                act.dma_start(w_up[0:MUL, 0:MUL], Wus).then_inc(up_loaded, 16)
                for i in range(3):
                    b = slice(MUL * (i + 1), MUL * (i + 2))
                    act.dma_start(w_up[b, b], Wuv).then_inc(up_loaded, 16)

                def relu(c):
                    for k, (t0, nt) in enumerate(PIECES):
                        act.wait_ge(centered, 2 * c + k + 1)
                        if c >= 2:
                            act.wait_ge(up_done, 2 * (c - 2) + k + 1)
                        act.activation(relu_c[:, c % 2, t0 * P:(t0 + nt) * P], psc[:, k, 0:nt * P],
                                       ACT.Relu).then_inc(relu_done, 1)
                    n = slice(c * CT, (c + 1) * CT)
                    act.wait_ge(stats_step, 5 * (c + 1))
                    act.activation(std[:, n], var_eps[:, n], ACT.Sqrt).then_inc(std_done, 1)

                def table_rows(c):
                    act.wait_ge(rstd_done, c + 1)
                    for k, (t0, nt) in enumerate(PIECES):
                        act.wait_ge(up_done, 2 * c + k + 1)
                        for t in range(nt):
                            n = c * CT + t0 + t
                            last = act.activation(tab_sb[:, n, :], psu[:, k, t * P:(t + 1) * P],
                                                  ACT.Copy, scale=rstd[:, n:n + 1])
                        last.then_inc(table_piece, 1)

                relu(0)
                for c in range(NCH):
                    if c + 1 < NCH:
                        relu(c + 1)
                    table_rows(c)

            @block.vector
            def _(dve):
                dve.wait_ge(up_loaded, 64)
                dve.tensor_scalar(w_up[:, :], w_up[:, :], float(MUL) ** -0.5, None, ALU.mult).then_inc(up_scaled, 1)
                dve.wait_ge(iota_built, 2)
                dve.tensor_copy(iota_f[:, :], iota_i[:, :]).then_inc(rounds_step, 1)

                def stats(c):
                    dve.wait_ge(x_loaded[c], 16)
                    for t in range(c * CT, (c + 1) * CT):
                        last = dve.bn_stats(bn[:, t, :], x_sb[:, t, :])
                    last.then_inc(bn_done, 1)
                    dve.wait_ge(bn_done, c + 1)
                    n = slice(c * CT, (c + 1) * CT)
                    dve.tensor_tensor(mean_gap[:, n], bn[:, n, 1], bn[:, n, 4], ALU.subtract).then_inc(stats_step, 1)
                    dve.tensor_tensor(m2_sum[:, n], bn[:, n, 2], bn[:, n, 5], ALU.add).then_inc(stats_step, 1)
                    dve.wait_ge(stats_step, 5 * c + 2)
                    dve.tensor_tensor(gap_sq[:, n], mean_gap[:, n], mean_gap[:, n], ALU.mult).then_inc(stats_step, 1)
                    dve.wait_ge(stats_step, 5 * c + 3)
                    dve.scalar_tensor_tensor(var_sum[:, n], gap_sq[:, n], F / 4.0, m2_sum[:, n],
                                             ALU.mult, ALU.add).then_inc(stats_step, 1)
                    dve.wait_ge(stats_step, 5 * c + 4)
                    dve.tensor_scalar(var_eps[:, n], var_sum[:, n], 1.0 / F, EPS, ALU.mult, ALU.add).then_inc(stats_step, 1)

                def invert(c):
                    n = slice(c * CT, (c + 1) * CT)
                    dve.wait_ge(std_done, c + 1)
                    dve.reciprocal(rstd[:, n], std[:, n]).then_inc(rstd_done, 1)

                stats(0)
                for c in range(NCH):
                    if c + 1 < NCH:
                        stats(c + 1)
                    invert(c)
                    if c == 3:
                        dve.wait_ge(dst_loaded, 16)
                        dve.tensor_reduce(group_stats[:, 0, :], dst_g, AX.X, ALU.min).then_inc(groups_reduced, 1)
                    if c == 4:
                        dve.tensor_reduce(group_stats[:, 1, :], dst_g, AX.X, ALU.max).then_inc(groups_reduced, 1)
                        dve.wait_ge(groups_reduced, 2)
                        dve.tensor_tensor(group_span[:, :], group_stats[:, 1, :], group_stats[:, 0, :],
                                          ALU.subtract).then_inc(groups_reduced, 1)
                dve.wait_ge(weights_loaded, 16 * N_WEIGHT_LOADS)
                dve.tensor_scalar(w_out[:, :, :], w_out[:, :, :], 0.1 * (2.0 * MUL) ** -0.5, None,
                                  ALU.mult).then_inc(out_scaled, 1)
                dve.wait_ge(out_scaled, 1)
                for i in range(3):
                    v = slice(MUL * (i + 1), MUL * (i + 2))
                    dve.tensor_scalar(w_out[v, 1 + i, 0:MUL], w_out[v, 1 + i, 0:MUL], 3.0 ** -0.5, None,
                                      ALU.mult).then_inc(out_scaled, 1)
                dve.wait_ge(groups_back, 48)
                dve.tensor_reduce(span_max[:, :], span_row[:, :], AX.X, ALU.max).then_inc(rounds_step, 1)
                dve.wait_ge(rounds_step, 2)
                dve.tensor_copy(span_int[:, :], span_max[:, :]).then_inc(rounds_step, 1)
                dve.wait_ge(rounds_step, 3)
                dve.tensor_scalar(span_windows[:, :], span_int[:, :], W.bit_length() - 1, None,
                                  ALU.arith_shift_right).then_inc(rounds_step, 1)
                dve.wait_ge(rounds_step, 4)
                dve.tensor_scalar(rounds_sb[:, :], span_windows[:, :], 1.0, float(MAX_ROUNDS),
                                  ALU.add, ALU.min).then_inc(rounds_step, 1)
                dve.wait_ge(out_scaled, 4)
                dve.wait_ge(rounds_step, 5)

            @block.tensor
            def _(pe):
                pe.wait_ge(center_built, 2)

                def center_chunk(c):
                    pe.wait_ge(xT_loaded[c], 16)
                    for k, (t0, nt) in enumerate(PIECES):
                        if c >= 1:
                            pe.wait_ge(relu_done, 2 * (c - 1) + k + 1)
                        n0 = (c * CT + t0) * P
                        nc.tensor.matmul(psc[:, k, 0:nt * P], center[:, :], xT_sb[:, n0:n0 + nt * P],
                                         start=True, stop=True).then_inc(centered, 1)

                def up_chunk(c):
                    for k, (t0, nt) in enumerate(PIECES):
                        pe.wait_ge(relu_done, 2 * c + k + 1)
                        if c >= 1:
                            pe.wait_ge(table_piece, 2 * (c - 1) + k + 1)
                        for t in range(nt):
                            last = nc.tensor.matmul(psu[:, k, t * P:(t + 1) * P],
                                                    relu_c[:, c % 2, (t0 + t) * P:(t0 + t + 1) * P],
                                                    w_up[:, :], start=True, stop=True)
                        last.then_inc(up_done, 1)

                center_chunk(0)
                pe.wait_ge(up_scaled, 1)
                for c in range(NCH):
                    if c + 1 < NCH:
                        center_chunk(c + 1)
                    up_chunk(c)

        rounds = nc.values_load(rounds_sb[0:1, 0:1], min_val=1, max_val=MAX_ROUNDS)
        with nc.Fori(0, rounds):
            with nc.Block() as block:

                @block.sync
                def _(sp):
                    def load_ef(j, b):
                        sp.dma_start(ef_in[:, b, :], efT[bass.ds(j * BODY + b, 1), :, :].rearrange("a p n -> (a p) n")
                                     ).then_inc(ef_loaded[b], 16)

                    def load_attr(j, b):
                        n = bass.ds(j * BODY + b, 1)
                        sp.dma_start(attr_in[:, b, :], attr[n, :, :].rearrange("a p n -> (a p) n")).then_inc(attr_loaded[b], 16)
                        sp.dma_start(dst_in[:, b, :], dst[n, :, :].rearrange("a p n -> (a p) n")).then_inc(attr_loaded[b], 16)

                    def load_src(j, b):
                        sp.dma_start(src_in[:, b, :], src[bass.ds(j * BODY + b, 1), :, :].rearrange("a p n -> (a p) n")
                                     ).then_inc(src_loaded[b], 16)

                    for b in range(BODY):
                        load_src(0, b)
                        load_ef(0, b)
                        load_attr(0, b)
                    with sp.Fori(0, NJ - 1) as j:
                        for b in range(BODY):
                            sp.wait_ge(gathered[b * QUADS + QUADS - 1], j * 16 * QT + 16 * QT)
                            load_src(j + 1, b)
                            sp.wait_ge(l1_done, j * 2 * BODY + 2 * b + 2)
                            load_ef(j + 1, b)
                            sp.wait_ge(onehot_ready, j * 2 * BODY + 2 * b + 2)
                            load_attr(j + 1, b)

                @block.gpsimd
                def _(pool):
                    pool.wait_ge(table_stored, 16 * NCH)

                    def gather(j, p, tiles=QT):
                        b, k = divmod(p, QUADS)
                        if k == 0:
                            pool.wait_ge(src_loaded[b], j * 16 + 16)
                        pool.wait_ge(msgs_ready, j * QB + p + 1)
                        pool.sem_inc(slots_claimed, 1)
                        for t in range(tiles):
                            at = QT * k + t
                            pool.indirect_dma_start(
                                out=rows[:, QT * p + t, :], out_offset=None, in_=table,
                                in_offset=bass.IndirectOffsetOnAxis(ap=src_in[:, b, at:at + 1], axis=0),
                            ).then_inc(gathered[p], 16)

                    with pool.Fori(0, NJ - 1) as j:
                        for p in range(QB):
                            gather(j, p)
                    for p in range(LAST_QUADS):
                        gather(NJ - 1, p, quad_tiles(p))
                    for p in range(QB):
                        pool.wait_ge(gathered[p], (NJ - 1) * 16 * QT + 16 * quad_tiles(p))
                    pool.dma_reset()

                @block.scalar
                def _(act):
                    act.sem_inc(h1_ready, HALF_CREDIT)
                    act.sem_inc(h2_ready, HALF_CREDIT)
                    act.sem_inc(sums_copied, SUMS_CREDIT)

                    def silu_1(m, h):
                        act.wait_ge(l1_done, m + 1)
                        act.wait_ge(l2_done, m + 1)
                        act.activation(h1[:, h, :], ps1[:, 0, :], ACT.Silu, bias=b1_sb[:, 0:1]).then_inc(h1_ready, 1)

                    def silu_2(m, h, b, quads_before):
                        act.wait_ge(l2_done, m + 1 + HALF_CREDIT)
                        act.wait_ge(w_ready, quads_before + QUADS)
                        act.activation(h2[:, b, h, :], ps2[:, 0, :], ACT.Silu, bias=b2_sb[:, 0:1]).then_inc(h2_ready, 1)

                    def silu(j, b, part):
                        m = j * 2 * BODY + 2 * b + part % 2
                        if part < 2:
                            silu_1(m, part)
                        else:
                            silu_2(m, part - 2, b, j * QB + b * QUADS)

                    def copy_sums(j, o, quads=2):
                        act.wait_ge(scatter_done, j * QB + 2 * o + quads + SCATTER_CREDIT)
                        act.wait_ge(out_ready, j * OCTS + o + 1)
                        act.activation(sums[:, o % 2, 0:2 * quads], pss[:, o % 2, 0:2 * quads], ACT.Copy).then_inc(sums_copied, 1)

                    def iteration(j, first=False, last=False):
                        for p in range(LAST_QUADS if last else QB):
                            b, k = divmod(p, QUADS)
                            if p % 2 == 0 and not (first and p == 0):
                                copy_sums(j, p // 2 - 1)
                            if b == 0:
                                silu(j, 1, k)
                            elif not last:
                                silu(j + 1, 0, k)

                    for part in range(4):
                        silu(0, 0, part)
                    iteration(0, first=True)
                    with act.Fori(1, NJ - 1) as j:
                        iteration(j)
                    iteration(NJ - 1, last=True)
                    copy_sums(NJ - 1, LAST_OCT, LAST_QUADS - 2 * LAST_OCT)

                @block.vector
                def _(dve):
                    dve.sem_inc(msgs_ready, MSG_CREDIT)
                    dve.sem_inc(window_added, ADD_CREDIT)
                    dve.tensor_scalar(start_now[:, :], start_all[:, :], offset[:, 0:1], None, ALU.add).then_inc(round_step, 1)
                    dve.tensor_scalar(span_row[:, :], start_row[:, :], offset[0:1, 0:1], float(NPAD),
                                      ALU.add, ALU.min).then_inc(round_step, 1)
                    dve.wait_ge(round_step, 2)
                    dve.tensor_scalar(start_at[:, :], span_row[:, :], 0.0, None, ALU.max).then_inc(round_step, 1)
                    dve.tensor_scalar(offset[:, :], offset[:, :], float(W), None, ALU.add).then_inc(round_step, 1)
                    dve.wait_ge(round_step, 4)

                    def relative(j, g):
                        b, h = divmod(g, 2)
                        dve.wait_ge(attr_loaded[b], j * 32 + 32)
                        dve.tensor_tensor(
                            rel[:, :].rearrange("p (w t) -> p w t", t=2),
                            dst_in[:, b, h * HT:(h + 1) * HT].rearrange("p (w t) -> p w t", t=2),
                            start_now[:, bass.ds(j * 2 * QB + g * HT // 2, HT // 2)].unsqueeze(2).broadcast_to([P, HT // 2, 2]),
                            ALU.subtract).then_inc(rel_ready, 1)

                    def equal(j, g):
                        dve.wait_ge(rel_ready, j * 4 + g + 1)
                        dve.tensor_tensor(eq[:, :, :], iota_f[:, :].unsqueeze(1).broadcast_to([P, HT, W]),
                                          rel[:, :].unsqueeze(2).broadcast_to([P, HT, W]),
                                          ALU.is_equal).then_inc(eq_ready, 1)

                    def scale(j, g):
                        b, h = divmod(g, 2)
                        dve.wait_ge(eq_ready, j * 4 + g + 1)
                        dve.tensor_tensor(
                            onehot[:, h, :, :, :],
                            eq[:, :, :].unsqueeze(2).broadcast_to([P, HT, 4, W]),
                            attr_in[:, b, h * 4 * HT:(h + 1) * 4 * HT].rearrange("p (t c) -> p t c", c=4)
                            .unsqueeze(3).broadcast_to([P, HT, 4, W]),
                            ALU.mult).then_inc(onehot_ready, 1)

                    def messages(j, p, tiles):
                        dve.wait_ge(gathered[p], j * 16 * QT + 16 * tiles)
                        dve.wait_ge(w_ready, j * QB + p + 1 + W_CREDIT)
                        dve.wait_ge(scatter_done, j * QB + p + 1)
                        g = rows[:, QT * p:QT * (p + 1), :].rearrange("p t (c u) -> p t c u", c=4)
                        m = msgs[:, p % SLOTS].rearrange("p t k (c u) -> p t k c u", c=4)
                        w = psw[:, p % SLOTS]
                        dve.tensor_tensor(m[:, :, :, 0, :], g[:, :, 0, :].unsqueeze(2).broadcast_to([P, QT, 2, MUL]),
                                          w[:, :, :, 0, :], ALU.mult)
                        dve.tensor_tensor(m[:, :, :, 1:4, :],
                                          g[:, :, 1:4, :].unsqueeze(2).broadcast_to([P, QT, 2, 3, MUL]),
                                          w[:, :, :, 1, :].unsqueeze(3).broadcast_to([P, QT, 2, 3, MUL]),
                                          ALU.mult).then_inc(msgs_ready, 1)

                    def add_window(j, n):
                        o, i = divmod(n, OW)
                        (start,) = nc.values_load_multi_w_load_instructions(
                            start_at[0:1, bass.ds(j * 2 * QB + n, 1)], engines=[mybir.EngineType.DVE],
                            min_val=0, max_val=NPAD,
                            skip_runtime_bounds_check_because="the round's first steps clamp the starts")[1]
                        if i == 0:
                            dve.wait_ge(out_ready, j * OCTS + o + 1 + OUT_CREDIT)
                        dve.wait_ge(window_added, j * 2 * QB + n + ADD_CREDIT)
                        at = xT_sb[:, bass.ds(start, W)]
                        dve.tensor_tensor(at, at, pso[:, o % 2, i * W:(i + 1) * W], ALU.add).then_inc(window_added, 1)

                    def iteration(j, first=False, last=False):
                        for p in range(LAST_QUADS if last else QB):
                            g = p // 2 + 1
                            ahead = (j + g // 4, g % 4) if not (last and 2 * g >= LAST_QUADS) else None
                            n = 2 * p - WINDOW_LAG
                            late = not (first and n < 0)
                            messages(j, p, quad_tiles(p) if last else QT)
                            if ahead and p % 2 == 0:
                                relative(*ahead)
                            if late:
                                add_window(j, n)
                            if ahead:
                                (equal, scale)[p % 2](*ahead)
                            if late:
                                add_window(j, n + 1)

                    relative(0, 0)
                    equal(0, 0)
                    scale(0, 0)
                    iteration(0, first=True)
                    with dve.Fori(1, NJ - 1) as j:
                        iteration(j)
                    iteration(NJ - 1, last=True)
                    for n in range(2 * LAST_QUADS - WINDOW_LAG, 2 * LAST_QUADS):
                        add_window(NJ - 1, n)

                @block.tensor
                def _(pe):
                    pe.sem_inc(scatter_done, SCATTER_CREDIT)
                    pe.sem_inc(w_ready, W_CREDIT)
                    pe.sem_inc(l2_done, HALF_CREDIT)
                    pe.sem_inc(out_ready, OUT_CREDIT)

                    def layer_1(j, b, h):
                        m = j * 2 * BODY + 2 * b + h
                        pe.wait_ge(ef_loaded[b], j * 16 + 16)
                        pe.wait_ge(h1_ready, m + HALF_CREDIT)
                        nc.tensor.matmul(ps1[:, 0, :], a1_bd[:, :], ef_in[:, b, h * MLP_HALF:(h + 1) * MLP_HALF],
                                         start=True, stop=True).then_inc(l1_done, 1)

                    def layer_2(j, b, h):
                        m = j * 2 * BODY + 2 * b + h
                        pe.wait_ge(h1_ready, m + 1 + HALF_CREDIT)
                        pe.wait_ge(h2_ready, m + HALF_CREDIT)
                        nc.tensor.matmul(ps2[:, 0, :], a2_bd[:, :], h1[:, h, :],
                                         start=True, stop=True).then_inc(l2_done, 1)

                    def layer_3(j, p):
                        b, k = divmod(p, QUADS)
                        h, c = divmod(2 * k, 4)
                        pe.wait_ge(h2_ready, j * 2 * BODY + 2 * b + h + 1 + HALF_CREDIT)
                        pe.wait_ge(msgs_ready, j * QB + p - 1 + MSG_CREDIT)
                        for i in range(2):
                            last = nc.tensor.matmul(
                                psw[:, p % SLOTS, 2 * i:2 * i + 2].rearrange("p b c d e -> p (b c d e)"),
                                h2[:, b, h, (c + i) * P:(c + i + 1) * P], a3_bd[:, :], start=True, stop=True)
                        last.then_inc(w_ready, 1)

                    def scatter(j, p):
                        g, k = divmod(p, 2)
                        pe.wait_ge(msgs_ready, j * QB + p + 1 + MSG_CREDIT)
                        pe.wait_ge(onehot_ready, j * 4 + g + 1)
                        o, q = divmod(p, 2)
                        if q == 0:
                            pe.wait_ge(sums_copied, j * OCTS + o + 1)
                        for i in range(2):
                            for part, c0, c1 in ((0, 0, 1), (1, 1, 4)):
                                for t in (2 * i, 2 * i + 1):
                                    last = nc.tensor.matmul(
                                        pss[:, o % 2, 2 * q + i, c0:c1, :].rearrange("p c w -> p (c w)"),
                                        msgs[:, p % SLOTS, t, part, :],
                                        onehot[:, g % 2, QT * k + t, c0:c1, :].rearrange("p c w -> p (c w)"),
                                        start=(t == 2 * i), stop=(t == 2 * i + 1))
                        last.then_inc(scatter_done, 1)

                    def project(j, o, quads=2):
                        pe.wait_ge(sums_copied, j * OCTS + o + 1 + SUMS_CREDIT)
                        pe.wait_ge(window_added, j * 2 * QB + OW * o + OW)
                        for c in range(4):
                            last = nc.tensor.matmul(pso[:, o % 2, 0:2 * quads * W], w_out[:, c, :],
                                                    sums[:, o % 2, 0:2 * quads, c, :],
                                                    start=(c == 0), stop=(c == 3))
                        last.then_inc(out_ready, 1)

                    def mlp_part(j, b, part):
                        (layer_1 if part < 2 else layer_2)(j, b, part % 2)

                    def iteration(j, first=False, last=False):
                        quads = LAST_QUADS if last else QB
                        for p in range(quads):
                            b, k = divmod(p, QUADS)
                            if p + 1 < quads:
                                layer_3(j, p + 1)
                            elif not last:
                                layer_3(j + 1, 0)
                            if b == 0:
                                mlp_part(j, 1, k)
                            elif not last:
                                mlp_part(j + 1, 0, k)
                            scatter(j, p)
                            if p % 2 == 0 and not (first and p == 0):
                                project(j, p // 2 - 1)

                    for part in range(4):
                        mlp_part(0, 0, part)
                    layer_3(0, 0)
                    iteration(0, first=True)
                    with pe.Fori(1, NJ - 1) as j:
                        iteration(j)
                    iteration(NJ - 1, last=True)
                    project(NJ - 1, LAST_OCT, LAST_QUADS - 2 * LAST_OCT)

            first_sem, last_sem = round_sems[0].num, round_sems[-1].num
            assert last_sem - first_sem == len(round_sems) - 1
            nc.all_engine_barrier(sems_to_clear=range(first_sem, last_sem + 1))

        with nc.Block() as block:

            @block.sync
            def _(sp):
                sp.dma_start(outT, xT_sb[:, 0:NPAD]).then_inc(out_stored, 16)
                sp.wait_ge(out_stored, 16)


FEATURES = np.concatenate([np.arange(MUL)] + [MUL + 3 * np.arange(MUL) + i for i in range(3)])
WEIGHT_COLUMNS = np.concatenate([MUL * k + np.arange(MUL) for k in (0, 2, 1, 3)])


def kernel(x, src, dst, edge_attr_4, edge_attr_8, L0_gnn_W_up_s, L0_gnn_W_up_v, L0_gnn_A1, L0_gnn_b1, L0_gnn_A2,
           L0_gnn_b2, L0_gnn_A3, L0_gnn_W_out_s, L0_gnn_W_out_v):
    import concourse.bacc as bacc
    from concourse.bass_utils import run_bass_kernel_spmd

    x, src, dst = np.asarray(x), np.asarray(src), np.asarray(dst)
    attr, ef = np.asarray(edge_attr_4), np.asarray(edge_attr_8)
    pad = EPAD - N_EDGES
    x_pad = np.pad(x, ((0, NPAD - N_NODES), (0, 0)))
    dst_pad = np.pad(dst, (0, pad), mode="edge")
    tiles = lambda a: np.ascontiguousarray(a.reshape(NB, TILES, P, -1).transpose(0, 2, 1, 3).reshape(NB, P, -1))
    arrays = {
        "x": x_pad,
        "xT": np.ascontiguousarray(x_pad[:, FEATURES].T),
        "src": tiles(np.pad(src, (0, pad))),
        "dst": tiles(dst_pad),
        "dst_groups": dst_pad.reshape(GP, NW // GP, GROUP),
        "attr": tiles(np.pad(attr, ((0, pad), (0, 0)))),
        "efT": np.ascontiguousarray(np.pad(ef, ((0, pad), (0, 0))).reshape(NB, TILES // 2, 2, P, EF)
                                    .transpose(0, 2, 4, 1, 3).reshape(NB, 2 * EF, BLOCK // 2)),
        "Wus": np.asarray(L0_gnn_W_up_s),
        "Wuv": np.asarray(L0_gnn_W_up_v),
        "A1": np.asarray(L0_gnn_A1),
        "b1": np.asarray(L0_gnn_b1).reshape(HID, 1),
        "A2": np.asarray(L0_gnn_A2),
        "b2": np.asarray(L0_gnn_b2).reshape(HID, 1),
        "A3": np.ascontiguousarray(np.asarray(L0_gnn_A3)[:, WEIGHT_COLUMNS]),
        "Wos": np.asarray(L0_gnn_W_out_s),
        "Wov": np.asarray(L0_gnn_W_out_v),
    }
    nc = bacc.Bacc("TRN2", target_bir_lowering=False, num_devices=1)
    args = {n: nc.dram_tensor(f"in_{n}", a.shape, mybir.dt.from_np(a.dtype), kind="ExternalInput").ap()
            for n, a in arrays.items()}
    outT = nc.dram_tensor("out_T", (F, NPAD), F32, kind="ExternalOutput").ap()
    gnn_layer_kernel(nc, **args, outT=outT)
    r = run_bass_kernel_spmd(nc, [{f"in_{n}": a for n, a in arrays.items()}], core_ids=[0])
    got = r.results[0]["out_T"][:, :N_NODES].T
    out = np.empty((N_NODES, F), got.dtype)
    out[:, FEATURES] = got
    return out
```

```python
from contextlib import ExitStack

import numpy as np
import concourse.bass as bass
from concourse import mybir

F32, I32 = mybir.dt.float32, mybir.dt.int32
ALU, ACT, AX = mybir.AluOpType, mybir.ActivationFunctionType, mybir.AxisListType

P = 128
MUL = 32
F = 4 * MUL
HID = 64
EF = 8
N_NODES, N_EDGES = 6250, 200000
NT = -(-N_NODES // P)
NPAD = NT * P
CT = 7
NCH = NT // CT
PIECES = [(0, 4), (4, 3)]

GROUP = 2 * P
QT = 4
QUADS = 4
TILES = QT * QUADS
BLOCK = TILES * P
BODY = 2
QB = BODY * QUADS
NJ = -(-N_EDGES // (BLOCK * BODY))
NB = NJ * BODY
NW = NB * BLOCK // GROUP
HT = TILES // 2
EPAD = NB * BLOCK
W = 32
GP = 112
XW = NPAD + W
MAX_ROUNDS = NPAD // W + 1
SLOTS = 2
OCTS = QB // 2
OW = 4
WINDOW_LAG = 2 * OW
EPS = 1e-5
MLP_HALF = HT * P // 2

MLP_WEIGHT_LOADS = 2 * 5
OUT_WEIGHT_LOADS = 1 + 3 * 3
LAST_EDGES = N_EDGES - (NJ - 1) * BODY * BLOCK
LAST_TILES = -(-LAST_EDGES // P)
LAST_QUADS = -(-LAST_TILES // QT)
LAST_OCT = (LAST_QUADS - 1) // 2

MSG_CREDIT = QB
SCATTER_CREDIT = SLOTS
W_CREDIT = QB
SUMS_CREDIT = 2
OUT_CREDIT = 2
ADD_CREDIT = 2 * OW
HALF_CREDIT = 2


def quad_tiles(p):
    return max(0, min(QT, LAST_TILES - QT * p))


def gnn_layer_kernel(nc, x, xT, src, dst, dst_groups, attr, efT, Wus, Wuv, A1, b1, A2, b2, A3, Wos, Wov, outT):
    table = nc.dram_tensor("node_table", (NPAD, F), F32, kind="Internal").ap()
    starts_dram = nc.dram_tensor("window_starts", (1, NW), F32, kind="Internal").ap()
    spans_dram = nc.dram_tensor("window_spans", (1, NW), F32, kind="Internal").ap()

    ctx = ExitStack()
    with ctx:
        def sb(name, shape, dt=F32):
            return ctx.enter_context(nc.sbuf_tensor(name, shape, dt))

        def pb(name, shape):
            return ctx.enter_context(nc.psum_tensor(name, shape, F32))

        def sem(name):
            return ctx.enter_context(nc.semaphore(name))

        xT_sb = sb("xT_sb", [P, XW])
        center = sb("center", [P, P])
        w_up = sb("w_up", [F, F])
        a1_bd = sb("a1_bd", [2 * EF, 2 * HID])
        a2_bd = sb("a2_bd", [2 * HID, 2 * HID])
        a3_bd = sb("a3_bd", [2 * HID, 2 * F])
        b1_sb = sb("b1_sb", [2 * HID, 1])
        b2_sb = sb("b2_sb", [2 * HID, 1])
        w_out = sb("w_out", [F, 4, F])
        iota_i = sb("iota_i", [P, W], I32)
        iota_f = sb("iota_f", [P, W])
        start_row = sb("start_row", [1, NW])
        start_at = sb("start_at", [1, NW], I32)
        start_all = sb("start_all", [P, NW])
        start_now = sb("start_now", [P, NW])
        span_row = sb("span_row", [1, NW])
        span_max = sb("span_max", [1, 1])
        span_int = sb("span_int", [1, 1], I32)
        span_windows = sb("span_windows", [1, 1], I32)
        rounds_sb = sb("rounds_sb", [1, 1], I32)
        offset = sb("offset", [P, 1])
        warm = sb("warm", [P, 1])
        group_stats = sb("group_stats", [GP, 2, NW // GP])
        group_span = sb("group_span", [GP, NW // GP])
        bn = sb("bn", [P, NT, 6])
        mean_gap = sb("mean_gap", [P, NT])
        gap_sq = sb("gap_sq", [P, NT])
        m2_sum = sb("m2_sum", [P, NT])
        var_sum = sb("var_sum", [P, NT])
        scaled_eps = sb("scaled_eps", [P, 1])
        std = sb("std", [P, NT])
        rstd = sb("rstd", [P, NT])
        rows = sb("rows", [P, QT * QB, F])
        msgs = sb("msgs", [P, SLOTS, QT, 2, F])
        onehot = sb("onehot", [P, 2, HT, 4, W])
        eq = sb("eq", [P, HT, W])
        rel = sb("rel", [P, HT])
        sums = sb("sums", [P, 2, OW, 4, W])
        h1 = sb("h1", [2 * HID, 2, MLP_HALF])
        h2 = sb("h2", [2 * HID, BODY, 2, MLP_HALF])
        ef_in = sb("ef_in", [2 * EF, BODY, 2 * MLP_HALF])
        attr_in = sb("attr_in", [P, BODY, TILES * 4])
        dst_in = sb("dst_in", [P, BODY, TILES], I32)
        src_in = sb("src_in", [P, BODY, TILES], I32)
        x_sb = sb("x_sb", [P, NT, F])
        tab_sb = sb("tab_sb", [P, NT, F])
        relu_c = msgs[:].rearrange("p a b c d -> p (a b c d)")[:, 0:2 * CT * P].rearrange("p (b n) -> p b n", b=2)
        dst_g = h2[:].rearrange("p a b c -> p (a b c)")[0:GP, 0:NW // GP * GROUP].bitcast(I32).rearrange("p (g e) -> p g e", e=GROUP)

        ps1 = pb("ps1", [P, 1, 512])
        ps2 = pb("ps2", [P, 1, 512])
        psw = pb("psw", [P, SLOTS, QT, 2, 2, MUL])
        pss = pb("pss", [P, 2, OW, 4, W])
        pso = pb("pso", [P, 2, 512])
        psc = psw[:].rearrange("p a b c d e -> p a (b c d e)")
        psu = [pss[:].rearrange("p a b c d -> p a (b c d)"), pso]

        dst_loaded = sem("dst_loaded")
        xT_loaded = [sem(f"xT_loaded{c}") for c in range(NCH)]
        x_loaded = [sem(f"x_loaded{c}") for c in range(NCH)]
        weights_zeroed = sem("weights_zeroed")
        up_loaded = sem("up_loaded")
        mlp_loaded = sem("mlp_loaded")
        out_loaded = sem("out_loaded")
        center_built = sem("center_built")
        iota_built = sem("iota_built")
        centered = sem("centered")
        relu_done = sem("relu_done")
        up_done = sem("up_done")
        table_piece = [sem(f"table_piece{k}") for k in range(len(PIECES))]
        stats_step = sem("stats_step")
        bn_done = sem("bn_done")
        std_done = sem("std_done")
        rstd_done = sem("rstd_done")
        table_stored = sem("table_stored")
        groups_reduced = sem("groups_reduced")
        groups_stored = sem("groups_stored")
        groups_back = sem("groups_back")
        rounds_step = sem("rounds_step")
        edge_zeroed = sem("edge_zeroed")
        out_scaled = sem("out_scaled")
        round_step = sem("round_step")
        ef_loaded = [sem(f"ef_loaded{b}") for b in range(BODY)]
        attr_loaded = [sem(f"attr_loaded{b}") for b in range(BODY)]
        src_loaded = [sem(f"src_loaded{b}") for b in range(BODY)]
        gathered = [sem(f"gathered{p}") for p in range(QB)]
        slots_claimed = sem("slots_claimed")
        l1_done = sem("l1_done")
        h1_ready = sem("h1_ready")
        l2_done = sem("l2_done")
        h2_ready = sem("h2_ready")
        w_ready = sem("w_ready")
        msgs_ready = sem("msgs_ready")
        rel_ready = sem("rel_ready")
        eq_ready = sem("eq_ready")
        onehot_ready = sem("onehot_ready")
        scatter_done = sem("scatter_done")
        sums_copied = sem("sums_copied")
        out_ready = sem("out_ready")
        window_added = sem("window_added")
        out_stored = sem("out_stored")

        round_sems = [round_step, *ef_loaded, *attr_loaded, *src_loaded, *gathered, slots_claimed, l1_done, h1_ready, l2_done,
                      h2_ready, w_ready, msgs_ready, rel_ready, eq_ready, onehot_ready, scatter_done, sums_copied, out_ready,
                      window_added]

        with nc.Block() as block:

            @block.sync
            def _(sp):
                for c in range(NCH):
                    cols = slice(c * CT * P, (c + 1) * CT * P)
                    sp.dma_start(xT_sb[:, cols], xT[:, cols]).then_inc(xT_loaded[c], 16)
                    sp.dma_start(x_sb[:, c * CT:(c + 1) * CT, :],
                                 x[cols, :].rearrange("(t p) f -> p t f", p=P)).then_inc(x_loaded[c], 16)
                    if c == 1:
                        sp.dma_start(dst_g, dst_groups).then_inc(dst_loaded, 16)

                def load_out_weights():
                    v = [slice(MUL * (i + 1), MUL * (i + 2)) for i in range(3)]
                    s = slice(0, MUL)
                    sp.dma_start(w_out[s, 0, s], Wos[0:MUL, :]).then_inc(out_loaded, 16)
                    for i in range(3):
                        sp.dma_start(w_out[v[i], 0, v[i]], Wov[MUL:2 * MUL, :]).then_inc(out_loaded, 16)
                        sp.dma_start(w_out[s, 1 + i, v[i]], Wov[0:MUL, :]).then_inc(out_loaded, 16)
                        sp.dma_start(w_out[v[i], 1 + i, s], Wos[MUL:2 * MUL, :]).then_inc(out_loaded, 16)

                sp.wait_ge(weights_zeroed, 5)
                for c in range(NCH):
                    for k, (t0, nt) in enumerate(PIECES):
                        t = c * CT + t0
                        sp.wait_ge(table_piece[k], c + 1)
                        sp.dma_start(table[t * P:(t + nt) * P, :].rearrange("(t p) f -> p t f", p=P),
                                     tab_sb[:, t:t + nt, :]).then_inc(table_stored, 16)
                    if c == 0:
                        load_out_weights()
                    if c == 1:
                        sp.wait_ge(groups_reduced, 3)
                        sp.dma_start(starts_dram.rearrange("a (p g) -> (a p) g", p=GP),
                                     group_stats[:, 0, :]).then_inc(groups_stored, 16)
                        sp.dma_start(spans_dram.rearrange("a (p g) -> (a p) g", p=GP),
                                     group_span[:, :]).then_inc(groups_stored, 16)
                    if c == 2:
                        sp.wait_ge(groups_stored, 32)
                        sp.dma_start(span_row[:, :], spans_dram).then_inc(groups_back, 16)
                        sp.dma_start(start_row[:, :], starts_dram).then_inc(groups_back, 16)
                        sp.dma_start(start_all[:, :], starts_dram.broadcast_to([P, NW])).then_inc(groups_back, 16)

            @block.gpsimd
            def _(pool):
                def variance(c):
                    pool.wait_ge(bn_done, c + 1)
                    n = slice(c * CT, (c + 1) * CT)
                    pool.tensor_tensor(mean_gap[:, n], bn[:, n, 1], bn[:, n, 4], ALU.subtract).then_inc(stats_step, 1)
                    pool.tensor_tensor(m2_sum[:, n], bn[:, n, 2], bn[:, n, 5], ALU.add).then_inc(stats_step, 1)
                    pool.wait_ge(stats_step, 5 * c + 1)
                    pool.tensor_tensor(gap_sq[:, n], mean_gap[:, n], mean_gap[:, n], ALU.mult).then_inc(stats_step, 1)
                    pool.wait_ge(stats_step, 5 * c + 3)
                    pool.tensor_scalar(gap_sq[:, n], gap_sq[:, n], F / 4.0, None, ALU.mult).then_inc(stats_step, 1)
                    pool.wait_ge(stats_step, 5 * c + 4)
                    pool.tensor_tensor(var_sum[:, n], gap_sq[:, n], m2_sum[:, n], ALU.add).then_inc(stats_step, 1)

                def load_mlp_matrices(g):
                    h = slice(HID * g, HID * (g + 1))
                    pool.dma_start(a1_bd[EF * g:EF * (g + 1), h], A1).then_inc(mlp_loaded, 16)
                    pool.dma_start(a2_bd[h, h], A2).then_inc(mlp_loaded, 16)
                    pool.dma_start(a3_bd[h, F * g:F * (g + 1)], A3).then_inc(mlp_loaded, 16)

                def load_mlp_biases(g):
                    h = slice(HID * g, HID * (g + 1))
                    pool.dma_start(b1_sb[h, :], b1).then_inc(mlp_loaded, 16)
                    pool.dma_start(b2_sb[h, :], b2).then_inc(mlp_loaded, 16)

                pool.memset(w_up[:, :], 0.0).then_inc(weights_zeroed, 1)
                pool.memset(center[:, :], -1.0 / P).then_inc(center_built, 1)
                pool.wait_ge(center_built, 1)
                pool.affine_select(out=center[:, :], in_=center[:, :], compare_op=ALU.not_equal, fill=1.0 - 1.0 / P,
                                   base=0, pattern=[[-1, P]], channel_multiplier=1).then_inc(center_built, 1)
                pool.iota(iota_i[:, :], pattern=[[1, W]], base=0, channel_multiplier=0).then_inc(iota_built, 1)
                pool.memset(offset[:, :], 0.0).then_inc(iota_built, 1)
                pool.memset(scaled_eps[:, :], MUL * EPS).then_inc(iota_built, 1)
                pool.memset(a1_bd[:, :], 0.0).then_inc(weights_zeroed, 1)
                pool.memset(a2_bd[:, :], 0.0).then_inc(weights_zeroed, 1)
                pool.memset(a3_bd[:, :], 0.0).then_inc(weights_zeroed, 1)
                pool.memset(w_out[:, :, :], 0.0).then_inc(weights_zeroed, 1)
                pool.memset(xT_sb[:, NPAD:XW], 0.0).then_inc(edge_zeroed, 1)
                pool.wait_ge(weights_zeroed, 5)
                load_mlp_matrices(0)
                for c in range(NCH):
                    variance(c)
                    if c == 1:
                        load_mlp_matrices(1)
                    if c == 2:
                        load_mlp_biases(0)
                    if c == 3:
                        load_mlp_biases(1)
                pool.wait_ge(out_loaded, 16 * OUT_WEIGHT_LOADS)
                pool.tensor_scalar(w_out[:, :, :], w_out[:, :, :], 0.1 * (2.0 * MUL) ** -0.5, None,
                                   ALU.mult).then_inc(out_scaled, 1)
                pool.wait_ge(out_scaled, 1)
                for i in range(3):
                    v = slice(MUL * (i + 1), MUL * (i + 2))
                    pool.tensor_scalar(w_out[v, 1 + i, 0:MUL], w_out[v, 1 + i, 0:MUL], 3.0 ** -0.5, None,
                                       ALU.mult).then_inc(out_scaled, 1)
                pool.wait_ge(out_scaled, 4)
                pool.wait_ge(edge_zeroed, 1)

            @block.scalar
            def _(act):
                act.wait_ge(weights_zeroed, 1)
                act.dma_start(w_up[0:MUL, 0:MUL], Wus).then_inc(up_loaded, 16)
                for i in range(3):
                    b = slice(MUL * (i + 1), MUL * (i + 2))
                    act.dma_start(w_up[b, b], Wuv).then_inc(up_loaded, 16)

                act.wait_ge(iota_built, 3)
                act.activation(warm[:, :], offset[:, :], ACT.Sqrt)

                def relu(c):
                    for k, (t0, nt) in enumerate(PIECES):
                        act.wait_ge(centered, 2 * c + k + 1)
                        if c >= 2:
                            act.wait_ge(up_done, 2 * (c - 2) + k + 1)
                        act.activation(relu_c[:, c % 2, t0 * P:(t0 + nt) * P], psc[:, k, 0:nt * P],
                                       ACT.Relu).then_inc(relu_done, 1)
                    n = slice(c * CT, (c + 1) * CT)
                    act.wait_ge(stats_step, 5 * (c + 1))
                    act.activation(std[:, n], var_sum[:, n], ACT.Sqrt, scale=MUL / F, bias=scaled_eps[:, 0:1]).then_inc(std_done, 1)

                def table_rows(c):
                    act.wait_ge(rstd_done, c + 1)
                    t0, nt = PIECES[0]
                    act.wait_ge(up_done, 2 * c + 1)
                    for t in range(c * CT + t0, c * CT + t0 + nt):
                        last = act.activation(tab_sb[:, t, :], psu[c % 2][:, 0, (t - c * CT) * P:(t - c * CT + 1) * P],
                                              ACT.Copy, scale=rstd[:, t:t + 1])
                    last.then_inc(table_piece[0], 1)

                relu(0)
                for c in range(NCH):
                    if c + 1 < NCH:
                        relu(c + 1)
                    table_rows(c)

            @block.vector
            def _(dve):
                dve.wait_ge(iota_built, 3)
                dve.tensor_copy(iota_f[:, :], iota_i[:, :]).then_inc(rounds_step, 1)

                def stats(c):
                    dve.wait_ge(x_loaded[c], 16)
                    for t in range(c * CT, (c + 1) * CT):
                        last = dve.bn_stats(bn[:, t, :], x_sb[:, t, :])
                    last.then_inc(bn_done, 1)

                def invert(c):
                    n = slice(c * CT, (c + 1) * CT)
                    dve.wait_ge(std_done, c + 1)
                    dve.reciprocal(rstd[:, n], std[:, n]).then_inc(rstd_done, 1)

                def table_rows(c):
                    t0, nt = PIECES[1]
                    n = slice(c * CT + t0, c * CT + t0 + nt)
                    dve.wait_ge(rstd_done, c + 1)
                    dve.wait_ge(up_done, 2 * c + 2)
                    dve.tensor_tensor(tab_sb[:, n, :], psu[c % 2][:, 1, 0:nt * P].rearrange("p (t f) -> p t f", f=F),
                                      rstd[:, n].unsqueeze(2).broadcast_to([P, nt, F]), ALU.mult).then_inc(table_piece[1], 1)

                def count_rounds():
                    dve.wait_ge(groups_back, 48)
                    dve.tensor_reduce(span_max[:, :], span_row[:, :], AX.X, ALU.max).then_inc(rounds_step, 1)
                    dve.wait_ge(rounds_step, 2)
                    dve.tensor_copy(span_int[:, :], span_max[:, :]).then_inc(rounds_step, 1)
                    dve.wait_ge(rounds_step, 3)
                    dve.tensor_scalar(span_windows[:, :], span_int[:, :], W.bit_length() - 1, None,
                                      ALU.arith_shift_right).then_inc(rounds_step, 1)
                    dve.wait_ge(rounds_step, 4)
                    dve.tensor_scalar(rounds_sb[:, :], span_windows[:, :], 1.0, float(MAX_ROUNDS),
                                      ALU.add, ALU.min).then_inc(rounds_step, 1)
                    dve.wait_ge(rounds_step, 5)

                stats(0)
                stats(1)
                invert(0)
                dve.wait_ge(dst_loaded, 16)
                dve.tensor_reduce(group_stats[:, 0, :], dst_g, AX.X, ALU.min).then_inc(groups_reduced, 1)
                for c in range(NCH):
                    table_rows(c)
                    if c + 2 < NCH:
                        stats(c + 2)
                    if c + 1 < NCH:
                        invert(c + 1)
                    if c == 1:
                        dve.tensor_reduce(group_stats[:, 1, :], dst_g, AX.X, ALU.max).then_inc(groups_reduced, 1)
                        dve.wait_ge(groups_reduced, 2)
                        dve.tensor_tensor(group_span[:, :], group_stats[:, 1, :], group_stats[:, 0, :],
                                          ALU.subtract).then_inc(groups_reduced, 1)
                count_rounds()

            @block.tensor
            def _(pe):
                pe.wait_ge(center_built, 2)

                def center_chunk(c):
                    pe.wait_ge(xT_loaded[c], 16)
                    for k, (t0, nt) in enumerate(PIECES):
                        if c >= 1:
                            pe.wait_ge(relu_done, 2 * (c - 1) + k + 1)
                        n0 = (c * CT + t0) * P
                        nc.tensor.matmul(psc[:, k, 0:nt * P], center[:, :], xT_sb[:, n0:n0 + nt * P],
                                         start=True, stop=True).then_inc(centered, 1)

                def up_chunk(c):
                    for k, (t0, nt) in enumerate(PIECES):
                        pe.wait_ge(relu_done, 2 * c + k + 1)
                        if c >= 2:
                            pe.wait_ge(table_piece[k], c - 1)
                        for t in range(nt):
                            last = nc.tensor.matmul(psu[c % 2][:, k, t * P:(t + 1) * P],
                                                    relu_c[:, c % 2, (t0 + t) * P:(t0 + t + 1) * P],
                                                    w_up[:, :], start=True, stop=True)
                        last.then_inc(up_done, 1)

                center_chunk(0)
                pe.wait_ge(up_loaded, 64)
                for c in range(NCH):
                    if c + 1 < NCH:
                        center_chunk(c + 1)
                    up_chunk(c)
                pe.wait_ge(mlp_loaded, 16 * MLP_WEIGHT_LOADS)

        rounds = nc.values_load(rounds_sb[0:1, 0:1], min_val=1, max_val=MAX_ROUNDS)
        with nc.Fori(0, rounds):
            with nc.Block() as block:

                @block.sync
                def _(sp):
                    def load_ef(j, b):
                        sp.dma_start(ef_in[:, b, :], efT[bass.ds(j * BODY + b, 1), :, :].rearrange("a p n -> (a p) n")
                                     ).then_inc(ef_loaded[b], 16)

                    def load_attr(j, b):
                        n = bass.ds(j * BODY + b, 1)
                        sp.dma_start(attr_in[:, b, :], attr[n, :, :].rearrange("a p n -> (a p) n")).then_inc(attr_loaded[b], 16)
                        sp.dma_start(dst_in[:, b, :], dst[n, :, :].rearrange("a p n -> (a p) n")).then_inc(attr_loaded[b], 16)

                    def load_src(j, b):
                        sp.dma_start(src_in[:, b, :], src[bass.ds(j * BODY + b, 1), :, :].rearrange("a p n -> (a p) n")
                                     ).then_inc(src_loaded[b], 16)

                    for b in range(BODY):
                        load_src(0, b)
                        load_ef(0, b)
                        load_attr(0, b)
                    with sp.Fori(0, NJ - 1) as j:
                        for b in range(BODY):
                            sp.wait_ge(gathered[b * QUADS + QUADS - 1], j * 16 * QT + 16 * QT)
                            load_src(j + 1, b)
                            sp.wait_ge(l1_done, j * 2 * BODY + 2 * b + 2)
                            load_ef(j + 1, b)
                            sp.wait_ge(onehot_ready, j * 2 * BODY + 2 * b + 2)
                            load_attr(j + 1, b)

                @block.gpsimd
                def _(pool):
                    pool.wait_ge(table_stored, 16 * NCH * len(PIECES))

                    def gather(j, p, tiles=QT):
                        b, k = divmod(p, QUADS)
                        if k == 0:
                            pool.wait_ge(src_loaded[b], j * 16 + 16)
                        pool.wait_ge(msgs_ready, j * QB + p + 1)
                        pool.sem_inc(slots_claimed, 1)
                        for t in range(tiles):
                            at = QT * k + t
                            pool.indirect_dma_start(
                                out=rows[:, QT * p + t, :], out_offset=None, in_=table,
                                in_offset=bass.IndirectOffsetOnAxis(ap=src_in[:, b, at:at + 1], axis=0),
                            ).then_inc(gathered[p], 16)

                    with pool.Fori(0, NJ - 1) as j:
                        for p in range(QB):
                            gather(j, p)
                    for p in range(LAST_QUADS):
                        gather(NJ - 1, p, quad_tiles(p))
                    for p in range(QB):
                        pool.wait_ge(gathered[p], (NJ - 1) * 16 * QT + 16 * quad_tiles(p))
                    pool.dma_reset()

                @block.scalar
                def _(act):
                    act.sem_inc(h1_ready, HALF_CREDIT)
                    act.sem_inc(h2_ready, HALF_CREDIT)
                    act.sem_inc(sums_copied, SUMS_CREDIT)

                    def silu_1(m, h):
                        act.wait_ge(l1_done, m + 1)
                        act.wait_ge(l2_done, m + 1)
                        act.activation(h1[:, h, :], ps1[:, 0, :], ACT.Silu, bias=b1_sb[:, 0:1]).then_inc(h1_ready, 1)

                    def silu_2(m, h, b, quads_before):
                        act.wait_ge(l2_done, m + 1 + HALF_CREDIT)
                        act.wait_ge(w_ready, quads_before + QUADS)
                        act.activation(h2[:, b, h, :], ps2[:, 0, :], ACT.Silu, bias=b2_sb[:, 0:1]).then_inc(h2_ready, 1)

                    def silu(j, b, part):
                        m = j * 2 * BODY + 2 * b + part % 2
                        if part < 2:
                            silu_1(m, part)
                        else:
                            silu_2(m, part - 2, b, j * QB + b * QUADS)

                    def copy_sums(j, o, quads=2):
                        act.wait_ge(scatter_done, j * QB + 2 * o + quads + SCATTER_CREDIT)
                        act.wait_ge(out_ready, j * OCTS + o + 1)
                        act.activation(sums[:, o % 2, 0:2 * quads], pss[:, o % 2, 0:2 * quads], ACT.Copy).then_inc(sums_copied, 1)

                    def iteration(j, first=False, last=False):
                        for p in range(LAST_QUADS if last else QB):
                            b, k = divmod(p, QUADS)
                            if p % 2 == 0 and not (first and p == 0):
                                copy_sums(j, p // 2 - 1)
                            if b == 0:
                                silu(j, 1, k)
                            elif not last:
                                silu(j + 1, 0, k)

                    for part in range(4):
                        silu(0, 0, part)
                    iteration(0, first=True)
                    with act.Fori(1, NJ - 1) as j:
                        iteration(j)
                    iteration(NJ - 1, last=True)
                    copy_sums(NJ - 1, LAST_OCT, LAST_QUADS - 2 * LAST_OCT)

                @block.vector
                def _(dve):
                    dve.sem_inc(msgs_ready, MSG_CREDIT)
                    dve.sem_inc(window_added, ADD_CREDIT)
                    dve.tensor_scalar(start_now[:, :], start_all[:, :], offset[:, 0:1], None, ALU.add).then_inc(round_step, 1)
                    dve.tensor_scalar(span_row[:, :], start_row[:, :], offset[0:1, 0:1], float(NPAD),
                                      ALU.add, ALU.min).then_inc(round_step, 1)
                    dve.wait_ge(round_step, 2)
                    dve.tensor_scalar(start_at[:, :], span_row[:, :], 0.0, None, ALU.max).then_inc(round_step, 1)
                    dve.tensor_scalar(offset[:, :], offset[:, :], float(W), None, ALU.add).then_inc(round_step, 1)
                    dve.wait_ge(round_step, 4)

                    def relative(j, g):
                        b, h = divmod(g, 2)
                        dve.wait_ge(attr_loaded[b], j * 32 + 32)
                        dve.tensor_tensor(
                            rel[:, :].rearrange("p (w t) -> p w t", t=2),
                            dst_in[:, b, h * HT:(h + 1) * HT].rearrange("p (w t) -> p w t", t=2),
                            start_now[:, bass.ds(j * 2 * QB + g * HT // 2, HT // 2)].unsqueeze(2).broadcast_to([P, HT // 2, 2]),
                            ALU.subtract).then_inc(rel_ready, 1)

                    def equal(j, g):
                        dve.wait_ge(rel_ready, j * 4 + g + 1)
                        dve.tensor_tensor(eq[:, :, :], iota_f[:, :].unsqueeze(1).broadcast_to([P, HT, W]),
                                          rel[:, :].unsqueeze(2).broadcast_to([P, HT, W]),
                                          ALU.is_equal).then_inc(eq_ready, 1)

                    def scale(j, g):
                        b, h = divmod(g, 2)
                        dve.wait_ge(eq_ready, j * 4 + g + 1)
                        dve.tensor_tensor(
                            onehot[:, h, :, :, :],
                            eq[:, :, :].unsqueeze(2).broadcast_to([P, HT, 4, W]),
                            attr_in[:, b, h * 4 * HT:(h + 1) * 4 * HT].rearrange("p (t c) -> p t c", c=4)
                            .unsqueeze(3).broadcast_to([P, HT, 4, W]),
                            ALU.mult).then_inc(onehot_ready, 1)

                    def messages(j, p, tiles):
                        dve.wait_ge(gathered[p], j * 16 * QT + 16 * tiles)
                        dve.wait_ge(w_ready, j * QB + p + 1 + W_CREDIT)
                        dve.wait_ge(scatter_done, j * QB + p + 1)
                        g = rows[:, QT * p:QT * (p + 1), :].rearrange("p t (c u) -> p t c u", c=4)
                        m = msgs[:, p % SLOTS].rearrange("p t k (c u) -> p t k c u", c=4)
                        w = psw[:, p % SLOTS]
                        dve.tensor_tensor(m[:, :, :, 0, :], g[:, :, 0, :].unsqueeze(2).broadcast_to([P, QT, 2, MUL]),
                                          w[:, :, :, 0, :], ALU.mult)
                        dve.tensor_tensor(m[:, :, :, 1:4, :],
                                          g[:, :, 1:4, :].unsqueeze(2).broadcast_to([P, QT, 2, 3, MUL]),
                                          w[:, :, :, 1, :].unsqueeze(3).broadcast_to([P, QT, 2, 3, MUL]),
                                          ALU.mult).then_inc(msgs_ready, 1)

                    def add_window(j, n):
                        o, i = divmod(n, OW)
                        (start,) = nc.values_load_multi_w_load_instructions(
                            start_at[0:1, bass.ds(j * 2 * QB + n, 1)], engines=[mybir.EngineType.DVE],
                            min_val=0, max_val=NPAD,
                            skip_runtime_bounds_check_because="the round's first steps clamp the starts")[1]
                        if i == 0:
                            dve.wait_ge(out_ready, j * OCTS + o + 1 + OUT_CREDIT)
                        dve.wait_ge(window_added, j * 2 * QB + n + ADD_CREDIT)
                        at = xT_sb[:, bass.ds(start, W)]
                        dve.tensor_tensor(at, at, pso[:, o % 2, i * W:(i + 1) * W], ALU.add).then_inc(window_added, 1)

                    def iteration(j, first=False, last=False):
                        for p in range(LAST_QUADS if last else QB):
                            g = p // 2 + 1
                            ahead = (j + g // 4, g % 4) if not (last and 2 * g >= LAST_QUADS) else None
                            n = 2 * p - WINDOW_LAG
                            late = not (first and n < 0)
                            messages(j, p, quad_tiles(p) if last else QT)
                            if ahead and p % 2 == 0:
                                relative(*ahead)
                            if late:
                                add_window(j, n)
                            if ahead:
                                (equal, scale)[p % 2](*ahead)
                            if late:
                                add_window(j, n + 1)

                    relative(0, 0)
                    equal(0, 0)
                    scale(0, 0)
                    iteration(0, first=True)
                    with dve.Fori(1, NJ - 1) as j:
                        iteration(j)
                    iteration(NJ - 1, last=True)
                    for n in range(2 * LAST_QUADS - WINDOW_LAG, 2 * LAST_QUADS):
                        add_window(NJ - 1, n)

                @block.tensor
                def _(pe):
                    pe.sem_inc(scatter_done, SCATTER_CREDIT)
                    pe.sem_inc(w_ready, W_CREDIT)
                    pe.sem_inc(l2_done, HALF_CREDIT)
                    pe.sem_inc(out_ready, OUT_CREDIT)

                    def layer_1(j, b, h):
                        m = j * 2 * BODY + 2 * b + h
                        pe.wait_ge(ef_loaded[b], j * 16 + 16)
                        pe.wait_ge(h1_ready, m + HALF_CREDIT)
                        nc.tensor.matmul(ps1[:, 0, :], a1_bd[:, :], ef_in[:, b, h * MLP_HALF:(h + 1) * MLP_HALF],
                                         start=True, stop=True).then_inc(l1_done, 1)

                    def layer_2(j, b, h):
                        m = j * 2 * BODY + 2 * b + h
                        pe.wait_ge(h1_ready, m + 1 + HALF_CREDIT)
                        pe.wait_ge(h2_ready, m + HALF_CREDIT)
                        nc.tensor.matmul(ps2[:, 0, :], a2_bd[:, :], h1[:, h, :],
                                         start=True, stop=True).then_inc(l2_done, 1)

                    def layer_3(j, p):
                        b, k = divmod(p, QUADS)
                        h, c = divmod(2 * k, 4)
                        pe.wait_ge(h2_ready, j * 2 * BODY + 2 * b + h + 1 + HALF_CREDIT)
                        pe.wait_ge(msgs_ready, j * QB + p - 1 + MSG_CREDIT)
                        for i in range(2):
                            last = nc.tensor.matmul(
                                psw[:, p % SLOTS, 2 * i:2 * i + 2].rearrange("p b c d e -> p (b c d e)"),
                                h2[:, b, h, (c + i) * P:(c + i + 1) * P], a3_bd[:, :], start=True, stop=True)
                        last.then_inc(w_ready, 1)

                    def scatter(j, p):
                        g, k = divmod(p, 2)
                        pe.wait_ge(msgs_ready, j * QB + p + 1 + MSG_CREDIT)
                        pe.wait_ge(onehot_ready, j * 4 + g + 1)
                        o, q = divmod(p, 2)
                        if q == 0:
                            pe.wait_ge(sums_copied, j * OCTS + o + 1)
                        for i in range(2):
                            for part, c0, c1 in ((0, 0, 1), (1, 1, 4)):
                                for t in (2 * i, 2 * i + 1):
                                    last = nc.tensor.matmul(
                                        pss[:, o % 2, 2 * q + i, c0:c1, :].rearrange("p c w -> p (c w)"),
                                        msgs[:, p % SLOTS, t, part, :],
                                        onehot[:, g % 2, QT * k + t, c0:c1, :].rearrange("p c w -> p (c w)"),
                                        start=(t == 2 * i), stop=(t == 2 * i + 1))
                        last.then_inc(scatter_done, 1)

                    def project(j, o, quads=2):
                        pe.wait_ge(sums_copied, j * OCTS + o + 1 + SUMS_CREDIT)
                        pe.wait_ge(window_added, j * 2 * QB + OW * o + OW)
                        for c in range(4):
                            last = nc.tensor.matmul(pso[:, o % 2, 0:2 * quads * W], w_out[:, c, :],
                                                    sums[:, o % 2, 0:2 * quads, c, :],
                                                    start=(c == 0), stop=(c == 3))
                        last.then_inc(out_ready, 1)

                    def mlp_part(j, b, part):
                        (layer_1 if part < 2 else layer_2)(j, b, part % 2)

                    def iteration(j, first=False, last=False):
                        quads = LAST_QUADS if last else QB
                        for p in range(quads):
                            b, k = divmod(p, QUADS)
                            if p + 1 < quads:
                                layer_3(j, p + 1)
                            elif not last:
                                layer_3(j + 1, 0)
                            if b == 0:
                                mlp_part(j, 1, k)
                            elif not last:
                                mlp_part(j + 1, 0, k)
                            ends = last and p == quads - 1
                            if not ends:
                                scatter(j, p)
                            if p % 2 == 0 and not (first and p == 0):
                                project(j, p // 2 - 1)
                            if ends:
                                scatter(j, p)

                    for part in range(4):
                        mlp_part(0, 0, part)
                    layer_3(0, 0)
                    iteration(0, first=True)
                    with pe.Fori(1, NJ - 1) as j:
                        iteration(j)
                    iteration(NJ - 1, last=True)
                    project(NJ - 1, LAST_OCT, LAST_QUADS - 2 * LAST_OCT)

            first_sem, last_sem = round_sems[0].num, round_sems[-1].num
            assert last_sem - first_sem == len(round_sems) - 1
            nc.all_engine_barrier(sems_to_clear=range(first_sem, last_sem + 1))

        with nc.Block() as block:

            @block.sync
            def _(sp):
                sp.dma_start(outT, xT_sb[:, 0:NPAD]).then_inc(out_stored, 16)
                sp.wait_ge(out_stored, 16)


FEATURES = np.concatenate([np.arange(MUL)] + [MUL + 3 * np.arange(MUL) + i for i in range(3)])
WEIGHT_COLUMNS = np.concatenate([MUL * k + np.arange(MUL) for k in (0, 2, 1, 3)])


def kernel(x, src, dst, edge_attr_4, edge_attr_8, L0_gnn_W_up_s, L0_gnn_W_up_v, L0_gnn_A1, L0_gnn_b1, L0_gnn_A2,
           L0_gnn_b2, L0_gnn_A3, L0_gnn_W_out_s, L0_gnn_W_out_v):
    import concourse.bacc as bacc
    from concourse.bass_utils import run_bass_kernel_spmd

    x, src, dst = np.asarray(x), np.asarray(src), np.asarray(dst)
    attr, ef = np.asarray(edge_attr_4), np.asarray(edge_attr_8)
    pad = EPAD - N_EDGES
    x_pad = np.pad(x, ((0, NPAD - N_NODES), (0, 0)))
    dst_pad = np.pad(dst, (0, pad), mode="edge")
    tiles = lambda a: np.ascontiguousarray(a.reshape(NB, TILES, P, -1).transpose(0, 2, 1, 3).reshape(NB, P, -1))
    arrays = {
        "x": x_pad,
        "xT": np.ascontiguousarray(x_pad[:, FEATURES].T),
        "src": tiles(np.pad(src, (0, pad))),
        "dst": tiles(dst_pad),
        "dst_groups": dst_pad.reshape(GP, NW // GP, GROUP),
        "attr": tiles(np.pad(attr, ((0, pad), (0, 0)))),
        "efT": np.ascontiguousarray(np.pad(ef, ((0, pad), (0, 0))).reshape(NB, TILES // 2, 2, P, EF)
                                    .transpose(0, 2, 4, 1, 3).reshape(NB, 2 * EF, BLOCK // 2)),
        "Wus": np.asarray(L0_gnn_W_up_s),
        "Wuv": np.asarray(L0_gnn_W_up_v),
        "A1": np.asarray(L0_gnn_A1),
        "b1": np.asarray(L0_gnn_b1).reshape(HID, 1),
        "A2": np.asarray(L0_gnn_A2),
        "b2": np.asarray(L0_gnn_b2).reshape(HID, 1),
        "A3": np.ascontiguousarray(np.asarray(L0_gnn_A3)[:, WEIGHT_COLUMNS]),
        "Wos": np.asarray(L0_gnn_W_out_s),
        "Wov": np.asarray(L0_gnn_W_out_v),
    }
    nc = bacc.Bacc("TRN2", target_bir_lowering=False, num_devices=1)
    args = {n: nc.dram_tensor(f"in_{n}", a.shape, mybir.dt.from_np(a.dtype), kind="ExternalInput").ap()
            for n, a in arrays.items()}
    outT = nc.dram_tensor("out_T", (F, NPAD), F32, kind="ExternalOutput").ap()
    gnn_layer_kernel(nc, **args, outT=outT)
    r = run_bass_kernel_spmd(nc, [{f"in_{n}": a for n, a in arrays.items()}], core_ids=[0])
    got = r.results[0]["out_T"][:, :N_NODES].T
    out = np.empty((N_NODES, F), got.dtype)
    out[:, FEATURES] = got
    return out
```
